# Optimizing a Trainium2 kernel written in Bass

```python
import numpy as np
import jax
import jax.numpy as jnp

def _softmax(x, axis=-1):
    return jax.nn.softmax(x, axis=axis)

def _gelu(x):
    return jax.nn.gelu(x, approximate=True)

def _silu(x):
    return jax.nn.silu(x)

def _sigmoid(x):
    return jax.nn.sigmoid(x)

def _layernorm(x, axis=-1, eps=1e-05):
    m = jnp.mean(x, axis=axis, keepdims=True)
    v = jnp.var(x, axis=axis, keepdims=True)
    return (x - m) / jnp.sqrt(v + eps)

def _scatter_add(tgt, idx, src, axis=0):
    return tgt.at[idx].add(src)

def _segment_sum(src, seg, n):
    return jax.ops.segment_sum(src, seg, n)
kernel_name = 'mk_seq_preln_d1_jaxref_r4_57722a'

def setup_inputs(seed: int=0):
    np.random.seed(seed)
    _w = jnp.asarray

    def _L0_attn_setup():
        import jax, jax.numpy as jnp
        import numpy as np
        HIDDEN, KEY_DIM, VALUE_DIM = (256, 256, 256)
        BATCH, SEQ = (8, 512)
        key = jax.random.key(seed)
        ks = jax.random.split(key, 9)
        s = lambda fan_in: 1.0 / np.sqrt(fan_in)
        return {'y_all': jax.random.normal(ks[0], (BATCH, SEQ, HIDDEN), dtype=jnp.float32), 'Wq': jax.random.uniform(ks[1], (HIDDEN, KEY_DIM), jnp.float32, -s(HIDDEN), s(HIDDEN)), 'bq': jax.random.uniform(ks[2], (KEY_DIM,), jnp.float32, -s(HIDDEN), s(HIDDEN)), 'Wk': jax.random.uniform(ks[3], (HIDDEN, KEY_DIM), jnp.float32, -s(HIDDEN), s(HIDDEN)), 'bk': jax.random.uniform(ks[4], (KEY_DIM,), jnp.float32, -s(HIDDEN), s(HIDDEN)), 'Wv': jax.random.uniform(ks[5], (HIDDEN, VALUE_DIM), jnp.float32, -s(HIDDEN), s(HIDDEN)), 'bv': jax.random.uniform(ks[6], (VALUE_DIM,), jnp.float32, -s(HIDDEN), s(HIDDEN)), 'Wo': jax.random.uniform(ks[7], (VALUE_DIM, HIDDEN), jnp.float32, -s(VALUE_DIM), s(VALUE_DIM)), 'bo': jax.random.uniform(ks[8], (HIDDEN,), jnp.float32, -s(VALUE_DIM), s(VALUE_DIM))}
    _L0_attn_in = _L0_attn_setup()

    def _L0_ffn_setup():
        import jax, jax.numpy as jnp
        import numpy as np
        DIM = 256

        def _reference_tuple_inner(x, W_r, W_k, W_v, mu_r, mu_k):
            B, T, C = x.shape
            x_prev = jnp.concatenate([jnp.zeros((B, 1, C), x.dtype), x[:, :-1, :]], axis=1)
            xr = mu_r * x + (1.0 - mu_r) * x_prev
            xk = mu_k * x + (1.0 - mu_k) * x_prev
            r = jax.nn.sigmoid(jnp.einsum('btc,dc->btd', xr, W_r))
            k = jnp.einsum('btc,dc->btd', xk, W_k)
            k_act = jnp.square(jax.nn.relu(k))
            out = r * jnp.einsum('btc,dc->btd', k_act, W_v)
            new_state = x[:, -1, :]
            return (out, new_state)
        key = jax.random.key(seed)
        ks = jax.random.split(key, 6)
        B, T, C = (8, 512, DIM)
        x = jax.random.normal(ks[0], (B, T, C), dtype=jnp.float32)
        s = 1.0 / np.sqrt(C)
        W_r = jax.random.uniform(ks[1], (C, C), jnp.float32, -s, s)
        W_k = jax.random.uniform(ks[2], (C, C), jnp.float32, -s, s)
        W_v = jax.random.uniform(ks[3], (C, C), jnp.float32, -s, s)
        mu_r = jax.random.uniform(ks[4], (C,), jnp.float32)
        mu_k = jax.random.uniform(ks[5], (C,), jnp.float32)
        return {'x': x, 'W_r': W_r, 'W_k': W_k, 'W_v': W_v, 'mu_r': mu_r, 'mu_k': mu_k}
    _L0_ffn_in = _L0_ffn_setup()
    _d = {'L0_attn_y_all': _L0_attn_in['y_all'], 'L0_attn_Wq': _L0_attn_in['Wq'], 'L0_attn_bq': _L0_attn_in['bq'], 'L0_attn_Wk': _L0_attn_in['Wk'], 'L0_attn_bk': _L0_attn_in['bk'], 'L0_attn_Wv': _L0_attn_in['Wv'], 'L0_attn_bv': _L0_attn_in['bv'], 'L0_attn_Wo': _L0_attn_in['Wo'], 'L0_attn_bo': _L0_attn_in['bo'], 'L0_ffn_W_r': _L0_ffn_in['W_r'], 'L0_ffn_W_k': _L0_ffn_in['W_k'], 'L0_ffn_W_v': _L0_ffn_in['W_v'], 'L0_ffn_mu_r': _L0_ffn_in['mu_r'], 'L0_ffn_mu_k': _L0_ffn_in['mu_k']}
    _x0 = _d['L0_attn_y_all']
    _d['L0_attn_y_all'] = jax.random.normal(jax.random.fold_in(jax.random.key(seed), 1), (2, 2048, 256), dtype=_x0.dtype)
    del _x0
    return _d

def reference(L0_attn_y_all, L0_attn_Wq, L0_attn_bq, L0_attn_Wk, L0_attn_bk, L0_attn_Wv, L0_attn_bv, L0_attn_Wo, L0_attn_bo, L0_ffn_W_r, L0_ffn_W_k, L0_ffn_W_v, L0_ffn_mu_r, L0_ffn_mu_k):

    def _L0_attn_ref(y_all, Wq, bq, Wk, bk, Wv, bv, Wo, bo):
        import jax, jax.numpy as jnp
        import numpy as np
        HIDDEN, KEY_DIM, VALUE_DIM = (256, 256, 256)
        BATCH, SEQ = (8, 512)
        B, T, H = y_all.shape
        dk = Wq.shape[1]
        q = (y_all @ Wq + bq) / jnp.sqrt(jnp.asarray(dk, y_all.dtype))
        k = y_all @ Wk + bk
        v = y_all @ Wv + bv
        scores = jnp.einsum('bid,bjd->bij', q, k)
        causal = jnp.tril(jnp.ones((T, T), dtype=bool))
        scores = jnp.where(causal, scores, -jnp.inf)
        weights = jax.nn.softmax(scores, axis=-1)
        ctx = jnp.einsum('bij,bjd->bid', weights, v)
        return ctx @ Wo + bo

    def _L0_ffn_ref(x, W_r, W_k, W_v, mu_r, mu_k):
        import jax, jax.numpy as jnp
        import numpy as np
        DIM = 256

        def _reference_tuple_inner(x, W_r, W_k, W_v, mu_r, mu_k):
            B, T, C = x.shape
            x_prev = jnp.concatenate([jnp.zeros((B, 1, C), x.dtype), x[:, :-1, :]], axis=1)
            xr = mu_r * x + (1.0 - mu_r) * x_prev
            xk = mu_k * x + (1.0 - mu_k) * x_prev
            r = jax.nn.sigmoid(jnp.einsum('btc,dc->btd', xr, W_r))
            k = jnp.einsum('btc,dc->btd', xk, W_k)
            k_act = jnp.square(jax.nn.relu(k))
            out = r * jnp.einsum('btc,dc->btd', k_act, W_v)
            new_state = x[:, -1, :]
            return (out, new_state)
        return _reference_tuple_inner(x, W_r, W_k, W_v, mu_r, mu_k)[0]
    x = L0_attn_y_all
    x = x + _L0_attn_ref(_layernorm(x, axis=-1), L0_attn_Wq, L0_attn_bq, L0_attn_Wk, L0_attn_bk, L0_attn_Wv, L0_attn_bv, L0_attn_Wo, L0_attn_bo)
    x = x + _L0_ffn_ref(_layernorm(x, axis=-1), L0_ffn_W_r, L0_ffn_W_k, L0_ffn_W_v, L0_ffn_mu_r, L0_ffn_mu_k)
    return x

_drawn_inputs = setup_inputs


def setup_inputs(seed=0):
    import zlib

    import numpy as np

    out = dict(_drawn_inputs(seed))
    spreads = {}
    factors = {'L0_attn_Wq': 6.078,
     'L0_attn_bq': 8.0,
     'L0_attn_Wk': 6.06,
     'L0_attn_bk': 64.0,
     'L0_ffn_W_r': 3.164,
     'L0_ffn_mu_r': 6.373,
     'L0_attn_bv': 2.752}
    for name, (base, spread) in spreads.items():
        noise = np.random.default_rng([zlib.crc32(name.encode()), seed]).standard_normal(out[name].shape)
        drawn = base * np.exp(spread * noise) if base else spread * noise
        out[name] = jnp.asarray(drawn.astype(out[name].dtype))
    for name, factor in factors.items():
        out[name] = (out[name] * factor).astype(out[name].dtype)
    return out
```

```python
import concourse.bass as bass
from concourse import mybir
from contextlib import ExitStack


def attention_channel_mix_block(nc, y, wq, bq, wk, bk, wv, bv, wo, bo, w_r, w_k, w_v, mu_r, mu_k, out):
    f32, f32r = mybir.dt.float32, mybir.dt.float32r
    ALU, ACT = mybir.AluOpType, mybir.ActivationFunctionType

    B, T, C = y.shape
    P = 128
    KC = C // P
    TG = 4
    GW = TG * P
    GB = T // GW
    NG = B * GB
    SCALE = float(C) ** -0.5
    MASKED = -3.0e38
    EPS = 1e-5

    STEPS = [[(c, p) for c in range(g + 1) for p in range(TG)] for g in (G % GB for G in range(NG))]
    FIRST = [sum(len(s) for s in STEPS[:G]) for G in range(NG + 1)]

    def width(G, c, p):
        return (p + 1) * P if c == G % GB else GW

    y_t = y.rearrange("b (n p) c -> p (b n) c", p=P)
    out_t = out.rearrange("b (n p) c -> p (b n) c", p=P)

    ctx = ExitStack()
    with ctx:
        def sb(name, shape, dt=f32):
            return ctx.enter_context(nc.sbuf_tensor(name, shape, dt))

        def sem(name):
            return ctx.enter_context(nc.semaphore(name))

        x_in = sb("x_in", [P, 2, TG, C])
        xhat = sb("xhat", [P, TG, C])
        o_sum = sb("o_sum", [P, TG, C])
        x1 = sb("x1", [P, TG, C])
        h_out = sb("h_out", [P, TG, C])
        sig = sb("sig", [P, TG, C])
        xT_hi, xT_lo = sb("xT_hi", [P, KC, GW], f32r), sb("xT_lo", [P, KC, GW], f32r)
        kT_hi, kT_lo = sb("kT_hi", [P, KC, T], f32r), sb("kT_lo", [P, KC, T], f32r)
        v_hi, v_lo = sb("v_hi", [P, T // P, C], f32r), sb("v_lo", [P, T // P, C], f32r)
        e_row = sb("e_row", [P, T])
        DIAG = [P * (p * (p + 1) // 2) for p in range(TG + 1)]
        e_diag = sb("e_diag", [P, DIAG[TG]])
        e_col = sb("e_col", [P, TG])
        prob = sb("prob", [P, 2, GW])
        pT_hi, pT_lo = sb("pT_hi", [P, 2, GW], f32r), sb("pT_lo", [P, 2, GW], f32r)
        hT = sb("hT", [P, 2, KC, GW + 1])
        mix = sb("mix", [P, 2 * KC, GW])
        mix_hi, mix_lo = sb("mix_hi", [P, 2 * KC, GW], f32r), sb("mix_lo", [P, 2 * KC, GW], f32r)
        act = sb("act", [P, KC, GW])
        act_hi, act_lo = sb("act_hi", [P, KC, GW], f32r), sb("act_lo", [P, KC, GW], f32r)
        wkq_hi, wkq_lo = sb("wkq_hi", [P, KC, C], f32r), sb("wkq_lo", [P, KC, C], f32r)
        wvo_hi, wvo_lo = sb("wvo_hi", [P, KC, C + 2], f32r), sb("wvo_lo", [P, KC, C + 2], f32r)
        ffn_hi, ffn_lo = sb("ffn_hi", [P, 3, KC, C], f32r), sb("ffn_lo", [P, 3, KC, C], f32r)
        cols = sb("cols", [P, 8, KC])
        BQ, BK, BV, MU_R, MU_K, OM_R, OM_K = range(7)
        smalls = sb("smalls", [P, 8])
        bkq = sb("bkq", [P, KC])
        e_const = sb("e_const", [P, 1])
        b_out = sb("b_out", [P, C])
        ident = sb("ident", [P, P])
        minus_half = sb("minus_half", [P, TG])
        stats = sb("stats", [P, TG, 6])
        mean_var = sb("mean_var", [P, TG, 2])
        var_eps = sb("var_eps", [P, TG])
        rstd = sb("rstd", [P, TG])
        stats2 = sb("stats2", [P, TG, 6])
        mean_var2 = sb("mean_var2", [P, TG, 2])
        var_eps2 = sb("var_eps2", [P, TG])
        rstd2 = sb("rstd2", [P, TG])
        row_max = sb("row_max", [P, 2, TG])
        neg_max = sb("neg_max", [P, TG])
        alpha = sb("alpha", [P, TG])
        row_sum = sb("row_sum", [P, TG])
        part_sum = sb("part_sum", [P, TG])
        inv_sum = sb("inv_sum", [P, TG])
        raw_k, raw_q = h_out[:, 0:2, :], h_out[:, 2:4, :]
        raw_v, raw_o = x1[:, 0:2, :], x1[:, 2:4, :]
        raw_ffn = mix[:, 0:3, :].rearrange("p m (k c) -> p m k c", k=KC)
        wkT = act[:, 0, :].rearrange("p (k c) -> p k c", k=KC)
        wqT = act[:, 1, :].rearrange("p (k c) -> p k c", k=KC)
        wvT = prob[:, 1, :].rearrange("p (k c) -> p k c", k=KC)
        bo_rows = sig[:, 0, :]

        bank_s, bank_p, bank_o, bank_g = [
            [ctx.enter_context(nc.psum_tensor(f"{n}{i}", [P, GW], f32)) for i in range(2)] for n in ("S", "PT", "O", "G")]
        ffn_bank = (bank_g[1], bank_s[0], bank_s[1])

        x_loaded = [sem(f"x_loaded{i}") for i in range(2)]
        (w_loaded, col_loaded, ffn_loaded, stored, const_ready, fold_ready, fold_moved, fold_split,
         bias_ready, ffn_ready, ffn_high, ffn_split, om_ready, stat1, var1_ready, eps1_ready, rstd1_ready, xhat_ready, xb_ready,
         xT_ready, xT_high, xT_split, kT_ready, kT_high, kT_split, v_ready, v_high, v_split, ecol_ready,
         e_ready, e_copied, mask_ready, s_ready, s_used, nmax_ready, exp_done, alpha_done, pT_ready, pT_high,
         pT_split, sum_done, inv_ready, o_ready, o_added, x1_ready, stat2, var2_ready, eps2_ready, rstd2_ready,
         h_ready, hT_ready, hT_copied, prev_ready, mu_done, mixed, mix_high, mix_split, k_ready, k_relu,
         squared, act_high, act_split, r_ready, r_exp, sig_plus, sig_ready, ff_ready, ff_used, out_ready) = [sem(n) for n in (
            "w_loaded col_loaded ffn_loaded stored const_ready fold_ready fold_moved fold_split "
            "bias_ready ffn_ready ffn_high ffn_split om_ready stat1 var1_ready eps1_ready rstd1_ready xhat_ready xb_ready "
            "xT_ready xT_high xT_split kT_ready kT_high kT_split v_ready v_high v_split ecol_ready "
            "e_ready e_copied mask_ready s_ready s_used nmax_ready exp_done alpha_done pT_ready pT_high "
            "pT_split sum_done inv_ready o_ready o_added x1_ready stat2 var2_ready eps2_ready rstd2_ready "
            "h_ready hT_ready hT_copied prev_ready mu_done mixed mix_high mix_split k_ready k_relu "
            "squared act_high act_split r_ready r_exp sig_plus sig_ready ff_ready ff_used out_ready").split()]

        block = ctx.enter_context(nc.Block())

        def halves(w):
            return w.rearrange("(k p) c -> p k c", p=P)

        def store(sp, G):
            for i in range(2):
                sp.wait_ge(out_ready, 2 * G + i + 1)
                t = G * TG + 2 * i
                sp.dma_start(out_t[:, t:t + 2, :], h_out[:, 2 * i:2 * i + 2, :]).then_inc(stored, 16)

        @block.sync
        def _(sp):
            sp.dma_start(raw_k, halves(wk)).then_inc(w_loaded, 16)
            sp.dma_start(raw_q, halves(wq)).then_inc(w_loaded, 16)
            sp.dma_start(x_in[:, 0], y_t[:, 0:TG, :]).then_inc(x_loaded[0], 16)
            sp.dma_start(raw_v, halves(wv)).then_inc(w_loaded, 16)
            sp.dma_start(raw_o, halves(wo)).then_inc(w_loaded, 16)
            sp.dma_start(bo_rows, bo.rearrange("(a c) -> a c", a=1).to_broadcast([P, C])).then_inc(w_loaded, 16)
            for i, w in enumerate((w_k, w_r, w_v)):
                sp.dma_start(raw_ffn[:, i], halves(w)).then_inc(ffn_loaded, 16)
            for G in range(1, NG + 1):
                if G < NG:
                    if G >= 2:
                        sp.wait_ge(x1_ready, TG * (G - 1))
                    sp.dma_start(x_in[:, G % 2], y_t[:, G * TG:(G + 1) * TG, :]).then_inc(x_loaded[G % 2], 16)
                if G >= 2:
                    store(sp, G - 2)
            store(sp, NG - 1)
            sp.wait_ge(stored, 32 * NG)

        @block.gpsimd
        def _(pool):
            g = nc.gpsimd
            g.memset(ident[:], 0.0).then_inc(const_ready, 1)
            g.memset(minus_half[:], -0.5).then_inc(const_ready, 1)
            pool.wait_ge(const_ready, 2)
            g.affine_select(out=ident[:], in_=ident[:], compare_op=ALU.not_equal, fill=1.0, base=0,
                            pattern=[[-1, P]], channel_multiplier=1).then_inc(const_ready, 1)

            def rsqrt(mv, ve, rs, ready, eps_done, done, G):
                pool.wait_ge(ready, G + 1)
                g.tensor_scalar(ve[:], mv[:, :, 1], EPS, None, ALU.add).then_inc(eps_done, 1)
                pool.wait_ge(eps_done, G + 1)
                g.tensor_tensor(rs[:], ve[:], minus_half[:], ALU.pow).then_inc(done, 1)

            def add_bias(G):
                pool.wait_ge(xhat_ready, G + 1)
                pool.wait_ge(bias_ready, 1)
                for t in range(TG):
                    last = g.tensor_tensor(x_in[:, G % 2, t, :], x_in[:, G % 2, t, :], b_out[:], ALU.add)
                last.then_inc(xb_ready, 1)

            rsqrt(mean_var, var_eps, rstd, var1_ready, eps1_ready, rstd1_ready, 0)
            add_bias(0)

            def add_and_release(G):
                for i in range(2):
                    pool.wait_ge(ff_used, 2 * G + i + 1)
                    s = slice(2 * i, 2 * i + 2)
                    g.tensor_tensor(h_out[:, s, :], h_out[:, s, :], x1[:, s, :], ALU.add).then_inc(out_ready, 1)

            for G in range(NG):
                pool.wait_ge(e_copied, G + 1)
                e0 = (G % GB) * GW
                for p in range(TG):
                    w = (p + 1) * P
                    g.affine_select(out=e_diag[:, DIAG[p]:DIAG[p] + w], in_=e_row[:, e0:e0 + w],
                                    compare_op=ALU.is_ge, fill=MASKED, base=p * P,
                                    pattern=[[-1, w]], channel_multiplier=1).then_inc(mask_ready, 1)
                if G > 0:
                    add_and_release(G - 1)
                if G + 1 < NG:
                    rsqrt(mean_var, var_eps, rstd, var1_ready, eps1_ready, rstd1_ready, G + 1)
                    add_bias(G + 1)
                rsqrt(mean_var2, var_eps2, rstd2, var2_ready, eps2_ready, rstd2_ready, G)
                for j in range(2 * KC):
                    pool.wait_ge(mix_high, 2 * KC * G + j + 1)
                    g.tensor_tensor(mix_lo[:, j], mix[:, j], mix_hi[:, j].bitcast(f32), ALU.subtract)\
                        .then_inc(mix_split, 1)
                for h in range(KC):
                    pool.wait_ge(act_high, KC * G + h + 1)
                    g.tensor_tensor(act[:, h], act[:, h], act[:, h], ALU.mult).then_inc(squared, 1)
                    pool.wait_ge(squared, KC * G + h + 1)
                    g.tensor_tensor(act_lo[:, h], act[:, h], act_hi[:, h].bitcast(f32), ALU.subtract)\
                        .then_inc(act_split, 1)
            add_and_release(NG - 1)

        @block.scalar
        def _(sc):
            a = nc.scalar
            with nc.allow_non_contiguous_dma(reason="vectors of 256 numbers, once"):
                for i, vec in enumerate((bq, bk, bv, mu_r, mu_k)):
                    sc.dma_start(cols[:, i, :], vec.rearrange("(k p) -> p k", p=P)).then_inc(col_loaded, 16)
            for i, (dst, src) in enumerate(((wkT, bank_g[0]), (wqT, bank_g[1]), (wvT, bank_s[0]))):
                sc.wait_ge(fold_ready, i + 1)
                a.activation(dst, src[:].rearrange("p (k c) -> p k c", k=KC), ACT.Copy).then_inc(fold_moved, 1)

            def high(dst, src, done, **kw):
                a.activation(dst, src, ACT.Copy, **kw).then_inc(done, 1)

            def xT_part(G, h):
                sc.wait_ge(xT_ready, KC * G + h + 1)
                high(xT_hi[:, h], bank_g[h][:], xT_high)

            def kT_part(G, h):
                sc.wait_ge(kT_ready, KC * G + h + 1)
                if G == 0 and h == 0:
                    sc.wait_ge(fold_split, 3)
                g0 = (G % GB) * GW
                a.activation(kT_hi[:, h, g0:g0 + GW], bank_s[h][:], ACT.Identity, bias=bkq[:, h:h + 1]).then_inc(kT_high, 1)

            def v_part(G, t):
                sc.wait_ge(v_ready, TG * G + t + 1)
                high(v_hi[:, (G % GB) * TG + t, :], (bank_p + bank_o)[t][:, 0:C], v_high)

            def e_part(G):
                sc.wait_ge(e_ready, G + 1)
                g0 = (G % GB) * GW
                high(e_row[:, g0:g0 + GW], bank_g[0][:], e_copied)

            for h in range(KC):
                xT_part(0, h)
            sc.wait_ge(fold_ready, 4)
            high(wkq_hi[:], bank_s[1][:].rearrange("p (k c) -> p k c", k=KC), fold_moved, scale=SCALE)
            sc.wait_ge(fold_ready, 5)
            for h in range(KC):
                high(wvo_hi[:, h, 0:C], (bank_o[0], bank_o[1])[h][:, 0:C], fold_moved)
            sc.wait_ge(fold_ready, 6)
            high(wvo_hi[:, :, C:C + 1], bank_p[0][:, 0:KC].rearrange("p (k a) -> p k a", a=1), fold_moved, scale=SCALE)
            for h in range(KC):
                kT_part(0, h)
            for t in range(TG):
                v_part(0, t)
            e_part(0)
            for i in range(3):
                sc.wait_ge(ffn_ready, i + 1)
                high(ffn_hi[:, i], ffn_bank[i][:].rearrange("p (k c) -> p k c", k=KC), ffn_high)

            for G in range(NG):
                steps, base = STEPS[G], FIRST[G]
                n = len(steps)
                for i in range(n + 1):
                    if i < n:
                        c, p = steps[i]
                        w = width(G, c, p)
                        s = base + i
                        sc.wait_ge(nmax_ready, s + 1)
                        acc = row_sum if c == 0 else part_sum
                        a.activation(prob[:, s % 2, 0:w], prob[:, s % 2, 0:w], ACT.Exp, bias=neg_max[:, p:p + 1],
                                     accum_out=acc[:, p:p + 1]).then_inc(exp_done, 1)
                        if c > 0:
                            a.activation(alpha[:, p:p + 1], row_max[:, (c - 1) % 2, p:p + 1], ACT.Exp,
                                         bias=neg_max[:, p:p + 1])
                    if i == n and G + 1 < NG:
                        xT_part(G + 1, 0)
                    if i >= 1:
                        c, p = steps[i - 1]
                        w = width(G, c, p)
                        s = base + i - 1
                        sc.wait_ge(pT_ready, s + 1)
                        high(pT_hi[:, s % 2, 0:w], bank_p[s % 2][:, 0:w], pT_high)
                    if i == n and G + 1 < NG:
                        xT_part(G + 1, 1)
                if G + 1 < NG:
                    for h in range(KC):
                        kT_part(G + 1, h)
                for h in range(KC):
                    sc.wait_ge(hT_ready, KC * G + h + 1)
                    high(hT[:, G % 2, h, 1:GW + 1], bank_g[h][:], hT_copied)

                def mu_part(j):
                    h, mu = j % KC, (MU_K, MU_R)[j // KC]
                    sc.wait_ge(hT_copied, KC * G + h + 1)
                    high(mix[:, j], hT[:, G % 2, h, 1:GW + 1], mu_done, scale=cols[:, mu, h:h + 1])

                def mix_part(j):
                    sc.wait_ge(mixed, 2 * KC * G + j + 1)
                    high(mix_hi[:, j], mix[:, j], mix_high)

                mu_part(0)
                mu_part(1)
                if G + 1 < NG:
                    v_part(G + 1, 0)
                    v_part(G + 1, 1)
                mix_part(0)
                mix_part(1)
                if G + 1 < NG:
                    v_part(G + 1, 2)
                    v_part(G + 1, 3)
                mu_part(2)
                mu_part(3)
                if G + 1 < NG:
                    e_part(G + 1)
                mix_part(2)
                mix_part(3)
                for h in range(KC):
                    sc.wait_ge(k_ready, KC * G + h + 1)
                    a.activation(act[:, h], bank_s[h][:], ACT.Relu).then_inc(k_relu, 1)
                    sc.wait_ge(k_relu, KC * G + h + 1)
                    a.activation(act_hi[:, h], act[:, h], ACT.Square).then_inc(act_high, 1)
                for i in range(2):
                    sc.wait_ge(r_ready, 2 * G + i + 1)
                    a.activation(sig[:, 2 * i:2 * i + 2, :], bank_g[i][:].rearrange("p (t c) -> p t c", c=C),
                                 ACT.Exp, scale=-1.0).then_inc(r_exp, 1)

        @block.vector
        def _(dve):
            v = nc.vector

            def low(dst, src, hi, done):
                v.tensor_tensor(dst, src, hi.bitcast(f32), ALU.subtract).then_inc(done, 1)

            def norm_stats(src, st, mv, t):
                v.bn_stats(st[:, t, :], src).then_inc(stat1 if st is stats else stat2, 1)

            def aggregate(st, mv, stat, done, G):
                dve.wait_ge(stat, TG * (G + 1))
                for t in range(TG):
                    last = v.bn_aggr(mv[:, t, :], st[:, t, :])
                last.then_inc(done, 1)

            def ln1(G, part):
                if part == 0:
                    dve.wait_ge(x_loaded[G % 2], 16 * (G // 2 + 1))
                    for t in range(TG):
                        v.bn_stats(stats[:, t, :], x_in[:, G % 2, t, :]).then_inc(stat1, 1)
                if part == 1:
                    aggregate(stats, mean_var, stat1, var1_ready, G)
                if part == 2:
                    dve.wait_ge(rstd1_ready, G + 1)
                    for t in range(TG):
                        last = v.tensor_scalar(xhat[:, t, :], x_in[:, G % 2, t, :], mean_var[:, t, 0:1],
                                               rstd[:, t:t + 1], ALU.subtract, ALU.mult)
                    last.then_inc(xhat_ready, 1)

            def xT_part(G, h):
                dve.wait_ge(xT_high, KC * G + h + 1)
                low(xT_lo[:, h], bank_g[h][:], xT_hi[:, h], xT_split)

            def kT_part(G, h):
                dve.wait_ge(kT_high, KC * G + h + 1)
                g0 = (G % GB) * GW
                v.scalar_tensor_tensor(kT_lo[:, h, g0:g0 + GW], bank_s[h][:], bkq[:, h:h + 1],
                                       kT_hi[:, h, g0:g0 + GW].bitcast(f32), ALU.add, ALU.subtract).then_inc(kT_split, 1)

            def v_part(G, t):
                dve.wait_ge(v_high, TG * G + t + 1)
                bank, tile = (bank_p + bank_o)[t], (G % GB) * TG + t
                last = v.tensor_scalar(e_col[:, t:t + 1], bank[:, C:C + 1], e_const[:, 0:1], None, ALU.add)
                if t == TG - 1:
                    last.then_inc(ecol_ready, 1)
                low(v_lo[:, tile, :], bank[:, 0:C], v_hi[:, tile, :], v_split)

            ln1(0, 0)
            ln1(0, 1)
            v.memset(wvo_hi[:, :, C:C + 2].bitcast(f32), 0.0).then_inc(om_ready, 1)
            v.memset(wvo_lo[:, :, C:C + 2].bitcast(f32), 0.0).then_inc(om_ready, 1)
            ln1(0, 2)
            dve.wait_ge(col_loaded, 80)
            v.tensor_scalar(cols[:, OM_R:OM_K + 1, :], cols[:, MU_R:MU_K + 1, :], -1.0, 1.0, ALU.mult, ALU.add)\
                .then_inc(om_ready, 1)
            for h in range(KC):
                xT_part(0, h)
            dve.wait_ge(fold_moved, 4)
            v.scalar_tensor_tensor(wkq_lo[:], bank_s[1][:].rearrange("p (k c) -> p k c", k=KC), SCALE,
                                   wkq_hi[:].bitcast(f32), ALU.mult, ALU.subtract).then_inc(fold_split, 1)
            dve.wait_ge(fold_moved, 6)
            for h in range(KC):
                last = v.tensor_tensor(wvo_lo[:, h, 0:C], bank_o[h][:, 0:C], wvo_hi[:, h, 0:C].bitcast(f32), ALU.subtract)
            dve.wait_ge(fold_moved, 7)
            v.scalar_tensor_tensor(wvo_lo[:, :, C:C + 1], bank_p[0][:, 0:KC].rearrange("p (k a) -> p k a", a=1), SCALE,
                                   wvo_hi[:, :, C:C + 1].bitcast(f32), ALU.mult, ALU.subtract).then_inc(fold_split, 1)
            v.tensor_scalar(e_const[:], bank_p[0][:, 2 * KC:2 * KC + 1], SCALE, None, ALU.mult)
            v.tensor_scalar(bkq[:], bank_p[0][:, KC:2 * KC], SCALE, None, ALU.mult).then_inc(fold_split, 1)
            dve.wait_ge(fold_ready, 7)
            v.tensor_tensor(b_out[:], bank_p[1][:, 0:C], bo_rows, ALU.add).then_inc(bias_ready, 1)
            for h in range(KC):
                kT_part(0, h)
            for t in range(TG):
                v_part(0, t)
            for i in range(3):
                dve.wait_ge(ffn_high, i + 1)
                low(ffn_lo[:, i], ffn_bank[i][:].rearrange("p (k c) -> p k c", k=KC), ffn_hi[:, i], ffn_split)

            def out_part(G):
                for i in range(2):
                    dve.wait_ge(ff_ready, 2 * G + i + 1)
                    dve.wait_ge(sig_ready, 2 * G + i + 1)
                    v.tensor_tensor(h_out[:, 2 * i:2 * i + 2, :], bank_g[i][:].rearrange("p (t c) -> p t c", c=C),
                                    sig[:, 2 * i:2 * i + 2, :], ALU.mult).then_inc(ff_used, 1)

            for G in range(NG):
                steps, base = STEPS[G], FIRST[G]
                n = len(steps)
                g = G % GB
                for i in range(n + 2):
                    if i < n:
                        c, p = steps[i]
                        w, s = width(G, c, p), base + i
                        if c == g:
                            dve.wait_ge(mask_ready, TG * G + p + 1)
                            e_s = e_diag[:, DIAG[p]:DIAG[p] + w]
                        else:
                            e_s = e_row[:, c * GW:c * GW + w]
                        dve.wait_ge(s_ready, s + 1)
                        before = MASKED if c == 0 else row_max[:, (c - 1) % 2, p:p + 1]
                        v.tensor_tensor_reduce(out=prob[:, s % 2, 0:w], in0=bank_s[s % 2][:, 0:w], in1=e_s, scale=1.0,
                                               scalar=before, op0=ALU.add, op1=ALU.max,
                                               accum_out=row_max[:, c % 2, p:p + 1]).then_inc(s_used, 1)
                        dve.wait_ge(s_used, s + 1)
                        v.tensor_scalar(neg_max[:, p:p + 1], row_max[:, c % 2, p:p + 1], -1.0, None, ALU.mult)\
                            .then_inc(nmax_ready, 1)
                    if i == 0 and G > 0:
                        out_part(G - 1)
                    if i == n and G + 1 < NG:
                        xT_part(G + 1, 0)
                    if 1 <= i <= n:
                        c, p = steps[i - 1]
                        w, s = width(G, c, p), base + i - 1
                        dve.wait_ge(pT_high, s + 1)
                        low(pT_lo[:, s % 2, 0:w], bank_p[s % 2][:, 0:w], pT_hi[:, s % 2, 0:w], pT_split)
                        if c > 0:
                            v.scalar_tensor_tensor(row_sum[:, p:p + 1], row_sum[:, p:p + 1], alpha[:, p:p + 1],
                                                   part_sum[:, p:p + 1], ALU.mult, ALU.add).then_inc(sum_done, 1)
                    if i == n and G + 1 < NG:
                        xT_part(G + 1, 1)
                    if i >= 2:
                        c, p = steps[i - 2]
                        s = base + i - 2
                        o = bank_o[s % 2][:, 0:C]
                        dve.wait_ge(o_ready, s + 1)
                        if c == 0:
                            v.tensor_copy(o_sum[:, p, :], o).then_inc(o_added, 1)
                        else:
                            v.scalar_tensor_tensor(o_sum[:, p, :], o_sum[:, p, :], alpha[:, p:p + 1], o,
                                                   ALU.mult, ALU.add).then_inc(o_added, 1)
                        if c == g:
                            v.reciprocal(inv_sum[:, p:p + 1], row_sum[:, p:p + 1]).then_inc(inv_ready, 1)
                            dve.wait_ge(inv_ready, TG * G + p + 1)
                            dve.wait_ge(o_added, s + 1)
                            if p == 0:
                                dve.wait_ge(xb_ready, G + 1)
                                if G > 0:
                                    dve.wait_ge(out_ready, 2 * G)
                            v.scalar_tensor_tensor(x1[:, p, :], o_sum[:, p, :], inv_sum[:, p:p + 1],
                                                   x_in[:, G % 2, p, :], ALU.mult, ALU.add).then_inc(x1_ready, 1)
                            dve.wait_ge(x1_ready, TG * G + p + 1)
                            v.bn_stats(stats2[:, p, :], x1[:, p, :]).then_inc(stat2, 1)
                    if G + 1 < NG and 1 <= i <= 3:
                        ln1(G + 1, i - 1)
                aggregate(stats2, mean_var2, stat2, var2_ready, G)
                if g == 0:
                    v.memset(hT[:, G % 2, :, 0:1], 0.0).then_inc(prev_ready, 1)
                else:
                    v.tensor_copy(hT[:, G % 2, :, 0:1], hT[:, (G - 1) % 2, :, GW:GW + 1]).then_inc(prev_ready, 1)
                dve.wait_ge(rstd2_ready, G + 1)
                if G > 0:
                    dve.wait_ge(stored, 32 * G)
                for t in range(TG):
                    last = v.tensor_scalar(h_out[:, t, :], x1[:, t, :], mean_var2[:, t, 0:1], rstd2[:, t:t + 1],
                                           ALU.subtract, ALU.mult)
                last.then_inc(h_ready, 1)
                if G + 1 < NG:
                    for h in range(KC):
                        kT_part(G + 1, h)

                def mix_part(j):
                    h, om = j % KC, (OM_K, OM_R)[j // KC]
                    dve.wait_ge(mu_done, 2 * KC * G + j + 1)
                    v.scalar_tensor_tensor(mix[:, j], hT[:, G % 2, h, 0:GW], cols[:, om, h:h + 1], mix[:, j],
                                           ALU.mult, ALU.add).then_inc(mixed, 1)

                dve.wait_ge(prev_ready, G + 1)
                mix_part(0)
                mix_part(1)
                if G + 1 < NG:
                    for t in range(TG):
                        v_part(G + 1, t)
                mix_part(2)
                mix_part(3)
                for i in range(2):
                    dve.wait_ge(r_exp, 2 * G + i + 1)
                    s = sig[:, 2 * i:2 * i + 2, :]
                    v.tensor_scalar(s, s, 1.0, None, ALU.add).then_inc(sig_plus, 1)
                    dve.wait_ge(sig_plus, 2 * G + i + 1)
                    v.reciprocal(s, s).then_inc(sig_ready, 1)
            out_part(NG - 1)

        @block.tensor
        def _(pe):
            mm = nc.tensor.matmul

            def product(dst, parts):
                last = None
                for n, (a_hi, a_lo, b_hi, b_lo) in enumerate(parts):
                    end = n == len(parts) - 1
                    mm(dst, a_hi, b_hi, start=n == 0, stop=False)
                    mm(dst, a_hi, b_lo, start=False, stop=False)
                    last = mm(dst, a_lo, b_hi, start=False, stop=end)
                return last

            def project(dst, w_hi, w_lo, cols_, x_hi, x_lo):
                return product(dst, [(w_hi[:, k, cols_], w_lo[:, k, cols_], x_hi[:, k, :], x_lo[:, k, :]) for k in range(KC)])

            def xT(G):
                pe.wait_ge(xhat_ready, G + 1)
                if G >= 2:
                    pe.wait_ge(ff_used, 2 * (G - 1))
                for h in range(KC):
                    for t in range(TG):
                        last = nc.tensor.transpose(bank_g[h][:, t * P:(t + 1) * P], xhat[:, t, h * P:(h + 1) * P], ident[:])
                    last.then_inc(xT_ready, 1)

            def kT(G):
                pe.wait_ge(xT_split, KC * (G + 1))
                for h in range(KC):
                    project(bank_s[h][:], wkq_hi, wkq_lo, slice(h * P, (h + 1) * P), xT_hi, xT_lo).then_inc(kT_ready, 1)

            def vv(G):
                if G > 0:
                    pe.wait_ge(o_added, FIRST[G])
                for t in range(TG):
                    rows = slice(t * P, (t + 1) * P)
                    product((bank_p + bank_o)[t][:, 0:C + 2],
                            [(xT_hi[:, k, rows], xT_lo[:, k, rows], wvo_hi[:, k, :], wvo_lo[:, k, :]) for k in range(KC)])\
                        .then_inc(v_ready, 1)

            def e(G):
                pe.wait_ge(ecol_ready, G + 1)
                if G > 0:
                    pe.wait_ge(hT_copied, KC * G)
                for t in range(TG):
                    last = nc.tensor.transpose(bank_g[0][:, t * P:(t + 1) * P], e_col[:, t:t + 1].to_broadcast([P, P]), ident[:])
                last.then_inc(e_ready, 1)

            def hTr(G):
                pe.wait_ge(h_ready, G + 1)
                for h in range(KC):
                    for t in range(TG):
                        last = nc.tensor.transpose(bank_g[h][:, t * P:(t + 1) * P], h_out[:, t, h * P:(h + 1) * P], ident[:])
                    last.then_inc(hT_ready, 1)

            def kk(G):
                pe.wait_ge(mix_split, 2 * KC * G + KC)
                if G + 1 < NG:
                    pe.wait_ge(kT_split, KC * (G + 2))
                for h in range(KC):
                    project(bank_s[h][:], ffn_hi[:, 0], ffn_lo[:, 0], slice(h * P, (h + 1) * P),
                            mix_hi[:, 0:KC], mix_lo[:, 0:KC]).then_inc(k_ready, 1)

            def rr(G):
                pe.wait_ge(mix_split, 2 * KC * (G + 1))
                if G + 1 < NG:
                    pe.wait_ge(e_copied, G + 2)
                for i in range(2):
                    for t in range(2 * i, 2 * i + 2):
                        rows = slice(t * P, (t + 1) * P)
                        last = product(bank_g[i][:, (t % 2) * C:(t % 2 + 1) * C],
                                       [(mix_hi[:, KC + k, rows], mix_lo[:, KC + k, rows], ffn_hi[:, 1, k, :], ffn_lo[:, 1, k, :])
                                        for k in range(KC)])
                    last.then_inc(r_ready, 1)

            def ff(G):
                pe.wait_ge(act_split, KC * (G + 1))
                pe.wait_ge(r_exp, 2 * (G + 1))
                for i in range(2):
                    for t in range(2 * i, 2 * i + 2):
                        rows = slice(t * P, (t + 1) * P)
                        last = product(bank_g[i][:, (t % 2) * C:(t % 2 + 1) * C],
                                       [(act_hi[:, k, rows], act_lo[:, k, rows], ffn_hi[:, 2, k, :], ffn_lo[:, 2, k, :])
                                        for k in range(KC)])
                    last.then_inc(ff_ready, 1)

            pe.wait_ge(const_ready, 3)
            for i, (raw, bank, need) in enumerate(((raw_k, bank_g[0], 32), (raw_q, bank_g[1], 32), (raw_v, bank_s[0], 80))):
                pe.wait_ge(w_loaded, need if i else 80)
                for d in range(KC):
                    for k in range(KC):
                        last = nc.tensor.transpose(bank[:, d * C + k * P:d * C + (k + 1) * P], raw[:, k, d * P:(d + 1) * P], ident[:])
                last.then_inc(fold_ready, 1)
            pe.wait_ge(fold_moved, 3)
            xT(0)
            for h in range(KC):
                for d in range(KC):
                    last = mm(bank_s[1][:, h * C:(h + 1) * C], wkT[:, d, h * P:(h + 1) * P], wqT[:, d, :], start=d == 0, stop=d == KC - 1)
            last.then_inc(fold_ready, 1)
            for h in range(KC):
                for d in range(KC):
                    last = mm(bank_o[h][:, 0:C], wvT[:, d, h * P:(h + 1) * P], raw_o[:, d, :], start=d == 0, stop=d == KC - 1)
            last.then_inc(fold_ready, 1)
            pe.wait_ge(col_loaded, 80)
            for dst, left, vec in ((0, wkT, BQ), (KC, wqT, BK)):
                for h in range(KC):
                    for d in range(KC):
                        last = mm(bank_p[0][:, dst + h:dst + h + 1], left[:, d, h * P:(h + 1) * P], cols[:, vec, d:d + 1],
                                  start=d == 0, stop=d == KC - 1)
            for d in range(KC):
                last = mm(bank_p[0][:, 2 * KC:2 * KC + 1], cols[:, BK, d:d + 1].to_broadcast([P, P]), cols[:, BQ, d:d + 1],
                          start=d == 0, stop=d == KC - 1)
            last.then_inc(fold_ready, 1)
            for d in range(KC):
                last = mm(bank_p[1][:, 0:C], cols[:, BV, d:d + 1].to_broadcast([P, P]), raw_o[:, d, :], start=d == 0, stop=d == KC - 1)
            last.then_inc(fold_ready, 1)
            pe.wait_ge(fold_split, 1)
            kT(0)
            pe.wait_ge(fold_split, 3)
            pe.wait_ge(bias_ready, 1)
            vv(0)
            e(0)
            pe.wait_ge(ffn_loaded, 48)
            for i in range(3):
                if i == 1:
                    pe.wait_ge(kT_split, KC)
                for k in range(KC):
                    for d in range(KC):
                        last = nc.tensor.transpose(ffn_bank[i][:, k * C + d * P:k * C + (d + 1) * P],
                                                   raw_ffn[:, i, d, k * P:(k + 1) * P], ident[:])
                last.then_inc(ffn_ready, 1)
            pe.wait_ge(ffn_split, 3)

            for G in range(NG):
                steps, base = STEPS[G], FIRST[G]
                n, g = len(steps), G % GB
                pe.wait_ge(kT_split, KC * (G + 1))
                if G > 0:
                    pe.wait_ge(k_relu, KC * G)
                for i in range(n + 2):
                    if i < n:
                        c, p = steps[i]
                        s, rows = base + i, slice(p * P, (p + 1) * P)
                        w = max(width(G, c, p), 2 * P)
                        keys = slice(c * GW, c * GW + w)
                        if i >= 2:
                            pe.wait_ge(s_used, s - 1)
                        product(bank_s[s % 2][:, 0:w],
                                [(xT_hi[:, k, rows], xT_lo[:, k, rows], kT_hi[:, k, keys], kT_lo[:, k, keys]) for k in range(KC)])\
                            .then_inc(s_ready, 1)
                    if i == 0 and G > 0:
                        ff(G - 1)
                    if i == n and G + 1 < NG:
                        xT(G + 1)
                    if 1 <= i <= n:
                        c, p = steps[i - 1]
                        s = base + i - 1
                        pe.wait_ge(exp_done, s + 1)
                        if i == 1:
                            pe.wait_ge(v_split, TG * (G + 1))
                        for b in range(width(G, c, p) // P):
                            last = nc.tensor.transpose(bank_p[s % 2][:, b * P:(b + 1) * P], prob[:, s % 2, b * P:(b + 1) * P], ident[:])
                        last.then_inc(pT_ready, 1)
                    if i >= 2:
                        c, p = steps[i - 2]
                        s = base + i - 2
                        pe.wait_ge(pT_split, s + 1)
                        if i >= 4:
                            pe.wait_ge(o_added, s - 1)
                        product(bank_o[s % 2][:, 0:C],
                                [(pT_hi[:, s % 2, b * P:(b + 1) * P], pT_lo[:, s % 2, b * P:(b + 1) * P],
                                  v_hi[:, c * TG + b, :], v_lo[:, c * TG + b, :]) for b in range(width(G, c, p) // P)])\
                            .then_inc(o_ready, 1)
                if G + 1 < NG:
                    kT(G + 1)
                hTr(G)
                if G + 1 < NG:
                    vv(G + 1)
                    e(G + 1)
                kk(G)
                rr(G)
            ff(NG - 1)


_INS = ["L0_attn_y_all", "L0_attn_Wq", "L0_attn_bq", "L0_attn_Wk", "L0_attn_bk", "L0_attn_Wv", "L0_attn_bv", "L0_attn_Wo",
        "L0_attn_bo", "L0_ffn_W_r", "L0_ffn_W_k", "L0_ffn_W_v", "L0_ffn_mu_r", "L0_ffn_mu_k"]


def kernel(**inputs):
    import numpy as _np
    import concourse.bacc as _bacc
    from concourse import mybir as _mybir
    from concourse.bass_utils import run_bass_kernel_spmd as _run

    nc = _bacc.Bacc("TRN2", target_bir_lowering=False, num_devices=1)
    arrays, args = {}, []
    for name in _INS:
        a = _np.ascontiguousarray(inputs[name])
        arrays[f"in_{name}_dram"] = a
        args.append(nc.dram_tensor(f"in_{name}_dram", a.shape, _mybir.dt.from_np(a.dtype), kind="ExternalInput").ap())
    shape = arrays["in_L0_attn_y_all_dram"].shape
    args.append(nc.dram_tensor("out_0_dram", shape, _mybir.dt.float32, kind="ExternalOutput").ap())
    attention_channel_mix_block(nc, *args)
    r = _run(nc, [arrays], core_ids=[0])
    return r.results[0]["out_0_dram"]
```

```python
import concourse.bass as bass
from concourse import mybir
from contextlib import ExitStack


def attention_channel_mix_block(nc, y, wq, bq, wk, bk, wv, bv, wo, bo, w_r, w_k, w_v, mu_r, mu_k, out):
    f32, f32r = mybir.dt.float32, mybir.dt.float32r
    ALU, ACT = mybir.AluOpType, mybir.ActivationFunctionType

    B, T, C = y.shape
    P = 128
    KC = C // P
    TG = 4
    GW = TG * P
    GB = T // GW
    NG = B * GB
    SCALE = float(C) ** -0.5
    MASKED = -3.0e38
    FFN_SCALE = (1.0, 1.0, 0.5)
    EPS = 1e-5

    STEPS = [[(c, p) for c in range(g + 1) for p in range(TG)] for g in (G % GB for G in range(NG))]
    FIRST = [sum(len(s) for s in STEPS[:G]) for G in range(NG + 1)]

    def width(G, c, p):
        return (p + 1) * P if c == G % GB else GW

    y_t = y.rearrange("b (n p) c -> p (b n) c", p=P)
    out_t = out.rearrange("b (n p) c -> p (b n) c", p=P)

    ctx = ExitStack()
    with ctx:
        def sb(name, shape, dt=f32):
            return ctx.enter_context(nc.sbuf_tensor(name, shape, dt))

        def sem(name):
            return ctx.enter_context(nc.semaphore(name))

        x_in = sb("x_in", [P, 2, TG, C])
        xhat = sb("xhat", [P, TG, C])
        o_sum = sb("o_sum", [P, TG, C])
        x1 = sb("x1", [P, TG, C])
        h_out = sb("h_out", [P, TG, C])
        gate = sb("gate", [P, TG, C])
        xT_hi, xT_lo = sb("xT_hi", [P, KC, GW], f32r), sb("xT_lo", [P, KC, GW], f32r)
        kT_hi, kT_lo = sb("kT_hi", [P, KC, T], f32r), sb("kT_lo", [P, KC, T], f32r)
        v_hi, v_lo = sb("v_hi", [P, T // P, C], f32r), sb("v_lo", [P, T // P, C], f32r)
        e_row = sb("e_row", [P, T])
        DIAG = [P * (p * (p + 1) // 2) for p in range(TG + 1)]
        e_diag = sb("e_diag", [P, DIAG[TG]])
        e_col = sb("e_col", [P, TG])
        prob = sb("prob", [P, 2, GW])
        pT_hi, pT_lo = sb("pT_hi", [P, 2, GW], f32r), sb("pT_lo", [P, 2, GW], f32r)
        hT = sb("hT", [P, 2, KC, GW + 1])
        mix = sb("mix", [P, 2 * KC, GW])
        mix_hi, mix_lo = sb("mix_hi", [P, 2 * KC, GW], f32r), sb("mix_lo", [P, 2 * KC, GW], f32r)
        act = sb("act", [P, KC, GW])
        relu = sb("relu", [P, GW])
        act_hi, act_lo = sb("act_hi", [P, KC, GW], f32r), sb("act_lo", [P, KC, GW], f32r)
        wkq_hi, wkq_lo = sb("wkq_hi", [P, KC, C], f32r), sb("wkq_lo", [P, KC, C], f32r)
        wvo_hi, wvo_lo = sb("wvo_hi", [P, KC, C + 2], f32r), sb("wvo_lo", [P, KC, C + 2], f32r)
        ffn_hi, ffn_lo = sb("ffn_hi", [P, 3, KC, C], f32r), sb("ffn_lo", [P, 3, KC, C], f32r)
        cols = sb("cols", [P, 8, KC])
        BQ, BK, BV, MU_R, MU_K, OM_R, OM_K = range(7)
        smalls = sb("smalls", [P, 8])
        bkq = sb("bkq", [P, KC])
        e_const = sb("e_const", [P, 1])
        b_out = sb("b_out", [P, C])
        ident = sb("ident", [P, P])
        minus_half = sb("minus_half", [P, TG])
        stats = sb("stats", [P, TG, 6])
        mean_var = sb("mean_var", [P, TG, 2])
        var_eps = sb("var_eps", [P, TG])
        rstd = sb("rstd", [P, TG])
        stats2 = sb("stats2", [P, TG, 6])
        mean_var2 = sb("mean_var2", [P, TG, 2])
        var_eps2 = sb("var_eps2", [P, TG])
        rstd2 = sb("rstd2", [P, TG])
        row_max = sb("row_max", [P, 2, TG])
        neg_max = sb("neg_max", [P, TG])
        alpha = sb("alpha", [P, TG])
        row_sum = sb("row_sum", [P, TG])
        part_sum = sb("part_sum", [P, TG])
        inv_sum = sb("inv_sum", [P, TG])
        raw_k, raw_q = h_out[:, 0:2, :], h_out[:, 2:4, :]
        raw_v, raw_o = x1[:, 0:2, :], x1[:, 2:4, :]
        raw_ffn = mix[:, 0:3, :].rearrange("p m (k c) -> p m k c", k=KC)
        wkT = act[:, 0, :].rearrange("p (k c) -> p k c", k=KC)
        wqT = act[:, 1, :].rearrange("p (k c) -> p k c", k=KC)
        wvT = prob[:, 1, :].rearrange("p (k c) -> p k c", k=KC)
        bo_rows = gate[:, 0, :]

        bank_s, bank_p, bank_o, bank_g = [
            [ctx.enter_context(nc.psum_tensor(f"{n}{i}", [P, GW], f32)) for i in range(2)] for n in ("S", "PT", "O", "G")]
        ffn_bank = (bank_g[0], bank_g[1], bank_g[0])

        x_loaded = [sem(f"x_loaded{i}") for i in range(2)]
        (w_loaded, col_loaded, ffn_loaded, stored, const_ready, fold_ready, fold_moved, fold_split,
         bias_ready, ffn_ready, ffn_high, ffn_split, om_ready, stat1, var1_ready, eps1_ready, rstd1_ready, xhat_ready, xb_ready,
         xT_ready, xT_high, xT_split, kT_ready, kT_high, kT_split, v_ready, v_high, v_split, ecol_ready,
         e_ready, e_copied, mask_ready, s_ready, s_used, nmax_ready, exp_done, alpha_done, pT_ready, pT_high,
         pT_split, sum_done, inv_ready, o_ready, o_added, x1_ready, stat2, var2_ready, eps2_ready, rstd2_ready,
         h_ready, hT_ready, hT_copied, prev_ready, mu_done, mixed, mix_high, xk_split, xr_split, k_ready, k_relu,
         squared, act_high, act_split, r_ready, gate_ready, ff_ready, ff_used, out_ready) = [sem(n) for n in (
            "w_loaded col_loaded ffn_loaded stored const_ready fold_ready fold_moved fold_split "
            "bias_ready ffn_ready ffn_high ffn_split om_ready stat1 var1_ready eps1_ready rstd1_ready xhat_ready xb_ready "
            "xT_ready xT_high xT_split kT_ready kT_high kT_split v_ready v_high v_split ecol_ready "
            "e_ready e_copied mask_ready s_ready s_used nmax_ready exp_done alpha_done pT_ready pT_high "
            "pT_split sum_done inv_ready o_ready o_added x1_ready stat2 var2_ready eps2_ready rstd2_ready "
            "h_ready hT_ready hT_copied prev_ready mu_done mixed mix_high xk_split xr_split k_ready k_relu "
            "squared act_high act_split r_ready gate_ready ff_ready ff_used out_ready").split()]

        block = ctx.enter_context(nc.Block())

        def halves(w):
            return w.rearrange("(k p) c -> p k c", p=P)

        def store(sp, G):
            for i in range(2):
                sp.wait_ge(out_ready, 2 * G + i + 1)
                t = G * TG + 2 * i
                sp.dma_start(out_t[:, t:t + 2, :], h_out[:, 2 * i:2 * i + 2, :]).then_inc(stored, 16)

        @block.sync
        def _(sp):
            sp.dma_start(raw_k, halves(wk)).then_inc(w_loaded, 16)
            sp.dma_start(raw_q, halves(wq)).then_inc(w_loaded, 16)
            sp.dma_start(x_in[:, 0], y_t[:, 0:TG, :]).then_inc(x_loaded[0], 16)
            sp.dma_start(raw_v, halves(wv)).then_inc(w_loaded, 16)
            sp.dma_start(raw_o, halves(wo)).then_inc(w_loaded, 16)
            sp.dma_start(bo_rows, bo.rearrange("(a c) -> a c", a=1).to_broadcast([P, C])).then_inc(w_loaded, 16)
            for i, w in enumerate((w_k, w_r, w_v)):
                sp.dma_start(raw_ffn[:, i], halves(w)).then_inc(ffn_loaded, 16)
            for G in range(1, NG + 1):
                if G < NG:
                    if G >= 2:
                        sp.wait_ge(x1_ready, TG * (G - 1))
                    sp.dma_start(x_in[:, G % 2], y_t[:, G * TG:(G + 1) * TG, :]).then_inc(x_loaded[G % 2], 16)
                if G >= 2:
                    store(sp, G - 2)
            store(sp, NG - 1)
            sp.wait_ge(stored, 32 * NG)

        @block.gpsimd
        def _(pool):
            g = nc.gpsimd
            g.memset(ident[:], 0.0).then_inc(const_ready, 1)
            g.memset(minus_half[:], -0.5).then_inc(const_ready, 1)
            pool.wait_ge(const_ready, 2)
            g.affine_select(out=ident[:], in_=ident[:], compare_op=ALU.not_equal, fill=1.0, base=0,
                            pattern=[[-1, P]], channel_multiplier=1).then_inc(const_ready, 1)

            def rsqrt(mv, ve, rs, ready, eps_done, done, count, tiles):
                pool.wait_ge(ready, count)
                g.tensor_scalar(ve[:, tiles], mv[:, tiles, 1], EPS, None, ALU.add).then_inc(eps_done, 1)
                pool.wait_ge(eps_done, count)
                g.tensor_tensor(rs[:, tiles], ve[:, tiles], minus_half[:, tiles], ALU.pow).then_inc(done, 1)

            def rsqrt1(G):
                rsqrt(mean_var, var_eps, rstd, var1_ready, eps1_ready, rstd1_ready, G + 1, slice(0, TG))

            def rsqrt2(G, p):
                rsqrt(mean_var2, var_eps2, rstd2, var2_ready, eps2_ready, rstd2_ready, TG * G + p + 1, slice(p, p + 1))

            def add_bias(G):
                pool.wait_ge(xhat_ready, TG * (G + 1))
                pool.wait_ge(bias_ready, 1)
                for t in range(TG):
                    last = g.tensor_tensor(x_in[:, G % 2, t, :], x_in[:, G % 2, t, :], b_out[:], ALU.add)
                last.then_inc(xb_ready, 1)

            rsqrt1(0)
            add_bias(0)

            def add_and_release(G):
                for i in range(2):
                    pool.wait_ge(ff_used, 2 * G + i + 1)
                    s = slice(2 * i, 2 * i + 2)
                    g.tensor_tensor(h_out[:, s, :], h_out[:, s, :], x1[:, s, :], ALU.add).then_inc(out_ready, 1)

            def masks(G):
                pool.wait_ge(e_copied, G + 1)
                e0 = (G % GB) * GW
                for p in range(TG):
                    w = (p + 1) * P
                    g.affine_select(out=e_diag[:, DIAG[p]:DIAG[p] + w], in_=e_row[:, e0:e0 + w],
                                    compare_op=ALU.is_ge, fill=MASKED, base=p * P,
                                    pattern=[[-1, w]], channel_multiplier=1).then_inc(mask_ready, 1)

            masks(0)
            for G in range(NG):
                if G > 0:
                    add_and_release(G - 1)
                if G + 1 < NG:
                    rsqrt1(G + 1)
                    add_bias(G + 1)
                for p in range(TG):
                    rsqrt2(G, p)
                if G + 1 < NG:
                    masks(G + 1)
                for h in range(KC):
                    j = KC + h
                    pool.wait_ge(mix_high, 2 * KC * G + j + 1)
                    g.tensor_tensor(mix_lo[:, j], mix[:, j], mix_hi[:, j].bitcast(f32), ALU.subtract)\
                        .then_inc(xr_split, 1)
            add_and_release(NG - 1)

        @block.scalar
        def _(sc):
            a = nc.scalar
            with nc.allow_non_contiguous_dma(reason="vectors of 256 numbers, once"):
                for i, vec in enumerate((bq, bk, bv, mu_r, mu_k)):
                    sc.dma_start(cols[:, i, :], vec.rearrange("(k p) -> p k", p=P)).then_inc(col_loaded, 16)
            for i, (dst, src) in enumerate(((wkT, bank_g[0]), (wqT, bank_g[1]), (wvT, bank_s[0]))):
                sc.wait_ge(fold_ready, i + 1)
                a.activation(dst, src[:].rearrange("p (k c) -> p k c", k=KC), ACT.Copy).then_inc(fold_moved, 1)

            def high(dst, src, done, **kw):
                a.activation(dst, src, ACT.Copy, **kw).then_inc(done, 1)

            def xT_part(G, h):
                sc.wait_ge(xT_ready, KC * G + h + 1)
                high(xT_hi[:, h], bank_g[h][:], xT_high)

            def kT_part(G, h):
                sc.wait_ge(kT_ready, KC * G + h + 1)
                if G == 0 and h == 0:
                    sc.wait_ge(fold_split, 3)
                g0 = (G % GB) * GW
                a.activation(kT_hi[:, h, g0:g0 + GW], bank_s[h][:], ACT.Identity, bias=bkq[:, h:h + 1]).then_inc(kT_high, 1)

            def v_part(G, t):
                sc.wait_ge(v_ready, TG * G + t + 1)
                high(v_hi[:, (G % GB) * TG + t, :], (bank_p + bank_o)[t][:, 0:C], v_high)

            def e_part(G):
                sc.wait_ge(e_ready, G + 1)
                g0 = (G % GB) * GW
                high(e_row[:, g0:g0 + GW], bank_p[0][:], e_copied)

            def exps(G, i):
                c, p = STEPS[G][i]
                w, s = width(G, c, p), FIRST[G] + i
                sc.wait_ge(nmax_ready, s + 1)
                acc = row_sum if c == 0 else part_sum
                a.activation(prob[:, s % 2, 0:w], prob[:, s % 2, 0:w], ACT.Exp, bias=neg_max[:, p:p + 1],
                             accum_out=acc[:, p:p + 1]).then_inc(exp_done, 1)
                if c > 0:
                    a.activation(alpha[:, p:p + 1], row_max[:, (c - 1) % 2, p:p + 1], ACT.Exp,
                                 bias=neg_max[:, p:p + 1])

            def pT_part(G, i):
                w, s = width(G, *STEPS[G][i]), FIRST[G] + i
                sc.wait_ge(pT_ready, s + 1)
                high(pT_hi[:, s % 2, 0:w], bank_p[s % 2][:, 0:w], pT_high)

            for h in range(KC):
                xT_part(0, h)
            sc.wait_ge(fold_ready, 4)
            high(wkq_hi[:], bank_s[1][:].rearrange("p (k c) -> p k c", k=KC), fold_moved, scale=SCALE)
            sc.wait_ge(fold_ready, 5)
            for h in range(KC):
                high(wvo_hi[:, h, 0:C], (bank_o[0], bank_o[1])[h][:, 0:C], fold_moved)
            sc.wait_ge(fold_ready, 6)
            high(wvo_hi[:, :, C:C + 1], bank_p[0][:, 0:KC].rearrange("p (k a) -> p k a", a=1), fold_moved, scale=SCALE)
            for h in range(KC):
                kT_part(0, h)
            for t in range(TG):
                v_part(0, t)
            e_part(0)
            exps(0, 0)
            exps(0, 1)
            for i in range(3):
                sc.wait_ge(ffn_ready, i + 1)
                high(ffn_hi[:, i], ffn_bank[i][:].rearrange("p (k c) -> p k c", k=KC), ffn_high, scale=FFN_SCALE[i])

            for G in range(NG):
                n = len(STEPS[G])
                for i in range(n + 1):
                    if i == n and G + 1 < NG:
                        xT_part(G + 1, 0)
                    if i >= 1:
                        pT_part(G, i - 1)
                    if i == n and G + 1 < NG:
                        xT_part(G + 1, 1)
                    if 2 <= i < n:
                        exps(G, i)
                if G + 1 < NG:
                    for h in range(KC):
                        kT_part(G + 1, h)
                    for t in range(TG):
                        v_part(G + 1, t)
                for h in range(KC):
                    sc.wait_ge(hT_ready, KC * G + h + 1)
                    high(hT[:, G % 2, h, 1:GW + 1], bank_g[h][:], hT_copied)

                def mu_part(j):
                    h, mu = j % KC, (MU_K, MU_R)[j // KC]
                    sc.wait_ge(hT_copied, KC * G + h + 1)
                    high(mix[:, j], hT[:, G % 2, h, 1:GW + 1], mu_done, scale=cols[:, mu, h:h + 1])

                def mix_part(j):
                    sc.wait_ge(mixed, 2 * KC * G + j + 1)
                    high(mix_hi[:, j], mix[:, j], mix_high)

                mu_part(0)
                mu_part(1)
                if G + 1 < NG:
                    e_part(G + 1)
                mix_part(0)
                mix_part(1)
                mu_part(2)
                mu_part(3)
                if G + 1 < NG:
                    exps(G + 1, 0)
                mix_part(2)
                if G + 1 < NG:
                    exps(G + 1, 1)
                mix_part(3)
                for h in range(KC):
                    sc.wait_ge(k_ready, KC * G + h + 1)
                    a.activation(relu[:], bank_g[h][:], ACT.Relu).then_inc(k_relu, 1)
                    sc.wait_ge(k_relu, KC * G + h + 1)
                    a.activation(act[:, h], relu[:], ACT.Square).then_inc(squared, 1)
                    sc.wait_ge(squared, KC * G + h + 1)
                    high(act_hi[:, h], act[:, h], act_high)
                for i in range(2):
                    sc.wait_ge(r_ready, 2 * G + i + 1)
                    a.activation(gate[:, 2 * i:2 * i + 2, :], bank_o[i][:].rearrange("p (t c) -> p t c", c=C),
                                 ACT.Tanh, scale=0.5).then_inc(gate_ready, 1)

        @block.vector
        def _(dve):
            v = nc.vector

            def low(dst, src, hi, done):
                v.tensor_tensor(dst, src, hi.bitcast(f32), ALU.subtract).then_inc(done, 1)

            def ln1_stats(G, t):
                if t == 0:
                    dve.wait_ge(x_loaded[G % 2], 16 * (G // 2 + 1))
                v.bn_stats(stats[:, t, :], x_in[:, G % 2, t, :]).then_inc(stat1, 1)

            def ln1_variance(G):
                dve.wait_ge(stat1, TG * (G + 1))
                for t in range(TG):
                    last = v.bn_aggr(mean_var[:, t, :], stats[:, t, :])
                last.then_inc(var1_ready, 1)

            def ln1_apply(G, t):
                if t == 0:
                    dve.wait_ge(rstd1_ready, G + 1)
                v.tensor_scalar(xhat[:, t, :], x_in[:, G % 2, t, :], mean_var[:, t, 0:1], rstd[:, t:t + 1],
                                ALU.subtract, ALU.mult).then_inc(xhat_ready, 1)

            def ln1_plan(n):
                if n == TG:
                    return {0: [(ln1_stats, 0), (ln1_stats, 1)], 1: [(ln1_stats, 2), (ln1_stats, 3), (ln1_variance,)],
                            2: [(ln1_apply, 0), (ln1_apply, 1)], 3: [(ln1_apply, 2), (ln1_apply, 3)]}
                plan = {t: [(ln1_stats, t)] for t in range(TG)}
                plan[TG - 1] += [(ln1_variance,)]
                return plan | {TG + t: [(ln1_apply, t)] for t in range(TG)}

            def xT_part(G, h):
                dve.wait_ge(xT_high, KC * G + h + 1)
                low(xT_lo[:, h], bank_g[h][:], xT_hi[:, h], xT_split)

            def kT_part(G, h):
                dve.wait_ge(kT_high, KC * G + h + 1)
                g0 = (G % GB) * GW
                v.scalar_tensor_tensor(kT_lo[:, h, g0:g0 + GW], bank_s[h][:], bkq[:, h:h + 1],
                                       kT_hi[:, h, g0:g0 + GW].bitcast(f32), ALU.add, ALU.subtract).then_inc(kT_split, 1)

            def v_part(G, t):
                dve.wait_ge(v_high, TG * G + t + 1)
                bank, tile = (bank_p + bank_o)[t], (G % GB) * TG + t
                last = v.tensor_scalar(e_col[:, t:t + 1], bank[:, C:C + 1], e_const[:, 0:1], None, ALU.add)
                if t == TG - 1:
                    last.then_inc(ecol_ready, 1)
                low(v_lo[:, tile, :], bank[:, 0:C], v_hi[:, tile, :], v_split)

            for t in range(TG):
                ln1_stats(0, t)
            ln1_variance(0)
            v.memset(wvo_hi[:, :, C:C + 2].bitcast(f32), 0.0).then_inc(om_ready, 1)
            v.memset(wvo_lo[:, :, C:C + 2].bitcast(f32), 0.0).then_inc(om_ready, 1)
            for t in range(TG):
                ln1_apply(0, t)
            dve.wait_ge(col_loaded, 80)
            v.tensor_scalar(cols[:, OM_R:OM_K + 1, :], cols[:, MU_R:MU_K + 1, :], -1.0, 1.0, ALU.mult, ALU.add)\
                .then_inc(om_ready, 1)
            for h in range(KC):
                xT_part(0, h)
            dve.wait_ge(fold_moved, 4)
            v.scalar_tensor_tensor(wkq_lo[:], bank_s[1][:].rearrange("p (k c) -> p k c", k=KC), SCALE,
                                   wkq_hi[:].bitcast(f32), ALU.mult, ALU.subtract).then_inc(fold_split, 1)
            dve.wait_ge(fold_moved, 6)
            for h in range(KC):
                last = v.tensor_tensor(wvo_lo[:, h, 0:C], bank_o[h][:, 0:C], wvo_hi[:, h, 0:C].bitcast(f32), ALU.subtract)
            dve.wait_ge(fold_moved, 7)
            v.scalar_tensor_tensor(wvo_lo[:, :, C:C + 1], bank_p[0][:, 0:KC].rearrange("p (k a) -> p k a", a=1), SCALE,
                                   wvo_hi[:, :, C:C + 1].bitcast(f32), ALU.mult, ALU.subtract).then_inc(fold_split, 1)
            v.tensor_scalar(e_const[:], bank_p[0][:, 2 * KC:2 * KC + 1], SCALE, None, ALU.mult)
            v.tensor_scalar(bkq[:], bank_p[0][:, KC:2 * KC], SCALE, None, ALU.mult).then_inc(fold_split, 1)
            dve.wait_ge(fold_ready, 7)
            v.tensor_tensor(b_out[:], bank_p[1][:, 0:C], bo_rows, ALU.add).then_inc(bias_ready, 1)
            for h in range(KC):
                kT_part(0, h)
            for t in range(TG):
                v_part(0, t)

            def scores(G, i):
                c, p = STEPS[G][i]
                w, s = width(G, c, p), FIRST[G] + i
                if c == G % GB:
                    dve.wait_ge(mask_ready, TG * G + p + 1)
                    e_s = e_diag[:, DIAG[p]:DIAG[p] + w]
                else:
                    e_s = e_row[:, c * GW:c * GW + w]
                dve.wait_ge(s_ready, s + 1)
                before = MASKED if c == 0 else row_max[:, (c - 1) % 2, p:p + 1]
                v.tensor_tensor_reduce(out=prob[:, s % 2, 0:w], in0=bank_s[s % 2][:, 0:w], in1=e_s, scale=1.0,
                                       scalar=before, op0=ALU.add, op1=ALU.max,
                                       accum_out=row_max[:, c % 2, p:p + 1]).then_inc(s_used, 1)
                dve.wait_ge(s_used, s + 1)
                v.tensor_scalar(neg_max[:, p:p + 1], row_max[:, c % 2, p:p + 1], -1.0, None, ALU.mult)\
                    .then_inc(nmax_ready, 1)

            def pT_part(G, i):
                c, p = STEPS[G][i]
                w, s = width(G, c, p), FIRST[G] + i
                dve.wait_ge(pT_high, s + 1)
                low(pT_lo[:, s % 2, 0:w], bank_p[s % 2][:, 0:w], pT_hi[:, s % 2, 0:w], pT_split)
                if c > 0:
                    v.scalar_tensor_tensor(row_sum[:, p:p + 1], row_sum[:, p:p + 1], alpha[:, p:p + 1],
                                           part_sum[:, p:p + 1], ALU.mult, ALU.add).then_inc(sum_done, 1)

            def o_part(G, i):
                c, p = STEPS[G][i]
                s = FIRST[G] + i
                o = bank_o[s % 2][:, 0:C]
                dve.wait_ge(o_ready, s + 1)
                if c == 0:
                    v.tensor_copy(o_sum[:, p, :], o).then_inc(o_added, 1)
                else:
                    v.scalar_tensor_tensor(o_sum[:, p, :], o_sum[:, p, :], alpha[:, p:p + 1], o,
                                           ALU.mult, ALU.add).then_inc(o_added, 1)
                if c == G % GB:
                    v.reciprocal(inv_sum[:, p:p + 1], row_sum[:, p:p + 1]).then_inc(inv_ready, 1)
                    dve.wait_ge(inv_ready, TG * G + p + 1)
                    dve.wait_ge(o_added, s + 1)
                    if p == 0:
                        dve.wait_ge(xb_ready, G + 1)
                        if G > 0:
                            dve.wait_ge(out_ready, 2 * G)
                    v.scalar_tensor_tensor(x1[:, p, :], o_sum[:, p, :], inv_sum[:, p:p + 1],
                                           x_in[:, G % 2, p, :], ALU.mult, ALU.add).then_inc(x1_ready, 1)
                    dve.wait_ge(x1_ready, TG * G + p + 1)
                    v.bn_stats(stats2[:, p, :], x1[:, p, :]).then_inc(stat2, 1)
                    dve.wait_ge(stat2, TG * G + p + 1)
                    v.bn_aggr(mean_var2[:, p, :], stats2[:, p, :]).then_inc(var2_ready, 1)

            def h_part(G, p):
                dve.wait_ge(rstd2_ready, TG * G + p + 1)
                if G > 0 and p == 0:
                    dve.wait_ge(stored, 32 * G)
                v.tensor_scalar(h_out[:, p, :], x1[:, p, :], mean_var2[:, p, 0:1], rstd2[:, p:p + 1],
                                ALU.subtract, ALU.mult).then_inc(h_ready, 1)

            def out_part(G):
                dve.wait_ge(gate_ready, 2 * (G + 1))
                for i in range(2):
                    dve.wait_ge(ff_ready, 2 * G + i + 1)
                    v.scalar_tensor_tensor(h_out[:, 2 * i:2 * i + 2, :].rearrange("p t c -> p (t c)"),
                                           gate[:, 2 * i:2 * i + 2, :].rearrange("p t c -> p (t c)"), 1.0, bank_g[i][:],
                                           ALU.add, ALU.mult).then_inc(ff_used, 1)

            scores(0, 0)
            scores(0, 1)
            for i in range(3):
                dve.wait_ge(ffn_high, i + 1)
                v.scalar_tensor_tensor(ffn_lo[:, i], ffn_bank[i][:].rearrange("p (k c) -> p k c", k=KC), FFN_SCALE[i],
                                       ffn_hi[:, i].bitcast(f32), ALU.mult, ALU.subtract).then_inc(ffn_split, 1)

            for G in range(NG):
                n, g = len(STEPS[G]), G % GB
                plan = ln1_plan(n) if G + 1 < NG else {}
                for i in range(n + 2):
                    if 2 <= i < n:
                        scores(G, i)
                    if i == n and G + 1 < NG:
                        xT_part(G + 1, 0)
                    if 1 <= i <= n:
                        pT_part(G, i - 1)
                    for what, *args_ in plan.get(i, ()):
                        what(G + 1, *args_)
                    if i == 1 and G > 0:
                        out_part(G - 1)
                    if i == n and G + 1 < NG:
                        xT_part(G + 1, 1)
                    if i >= 2:
                        o_part(G, i - 2)
                    if i >= n - 1:
                        h_part(G, i - (n - 1))
                if g == 0:
                    v.memset(hT[:, G % 2, :, 0:1], 0.0).then_inc(prev_ready, 1)
                else:
                    v.tensor_copy(hT[:, G % 2, :, 0:1], hT[:, (G - 1) % 2, :, GW:GW + 1]).then_inc(prev_ready, 1)
                if G + 1 < NG:
                    kT_part(G + 1, 0)
                h_part(G, TG - 1)
                if G + 1 < NG:
                    kT_part(G + 1, 1)
                    for t in range(TG):
                        v_part(G + 1, t)

                def mix_part(j):
                    h, om = j % KC, (OM_K, OM_R)[j // KC]
                    dve.wait_ge(mu_done, 2 * KC * G + j + 1)
                    v.scalar_tensor_tensor(mix[:, j], hT[:, G % 2, h, 0:GW], cols[:, om, h:h + 1], mix[:, j],
                                           ALU.mult, ALU.add).then_inc(mixed, 1)

                dve.wait_ge(prev_ready, G + 1)
                mix_part(0)
                mix_part(1)
                for h in range(KC):
                    dve.wait_ge(mix_high, 2 * KC * G + h + 1)
                    low(mix_lo[:, h], mix[:, h], mix_hi[:, h], xk_split)
                if G + 1 < NG:
                    scores(G + 1, 0)
                mix_part(2)
                if G + 1 < NG:
                    scores(G + 1, 1)
                mix_part(3)
                for h in range(KC):
                    dve.wait_ge(act_high, KC * G + h + 1)
                    low(act_lo[:, h], act[:, h], act_hi[:, h], act_split)
            out_part(NG - 1)

        @block.tensor
        def _(pe):
            mm = nc.tensor.matmul

            def product(dst, parts):
                last = None
                for n, (a_hi, a_lo, b_hi, b_lo) in enumerate(parts):
                    end = n == len(parts) - 1
                    mm(dst, a_hi, b_hi, start=n == 0, stop=False)
                    mm(dst, a_hi, b_lo, start=False, stop=False)
                    last = mm(dst, a_lo, b_hi, start=False, stop=end)
                return last

            def project(dst, w_hi, w_lo, cols_, x_hi, x_lo):
                return product(dst, [(w_hi[:, k, cols_], w_lo[:, k, cols_], x_hi[:, k, :], x_lo[:, k, :]) for k in range(KC)])

            def xT(G):
                pe.wait_ge(xhat_ready, TG * (G + 1))
                if G >= 2:
                    pe.wait_ge(ff_used, 2 * (G - 1))
                for h in range(KC):
                    for t in range(TG):
                        last = nc.tensor.transpose(bank_g[h][:, t * P:(t + 1) * P], xhat[:, t, h * P:(h + 1) * P], ident[:])
                    last.then_inc(xT_ready, 1)

            def kT(G):
                pe.wait_ge(xT_split, KC * (G + 1))
                for h in range(KC):
                    project(bank_s[h][:], wkq_hi, wkq_lo, slice(h * P, (h + 1) * P), xT_hi, xT_lo).then_inc(kT_ready, 1)

            def vv(G):
                if G > 0:
                    pe.wait_ge(o_added, FIRST[G])
                for t in range(TG):
                    rows = slice(t * P, (t + 1) * P)
                    product((bank_p + bank_o)[t][:, 0:C + 2],
                            [(xT_hi[:, k, rows], xT_lo[:, k, rows], wvo_hi[:, k, :], wvo_lo[:, k, :]) for k in range(KC)])\
                        .then_inc(v_ready, 1)

            def e(G):
                pe.wait_ge(ecol_ready, G + 1)
                pe.wait_ge(v_split, TG * (G + 1))
                for t in range(TG):
                    last = nc.tensor.transpose(bank_p[0][:, t * P:(t + 1) * P], e_col[:, t:t + 1].to_broadcast([P, P]), ident[:])
                last.then_inc(e_ready, 1)

            def hTr(G):
                pe.wait_ge(h_ready, TG * (G + 1))
                for h in range(KC):
                    for t in range(TG):
                        last = nc.tensor.transpose(bank_g[h][:, t * P:(t + 1) * P], h_out[:, t, h * P:(h + 1) * P], ident[:])
                    last.then_inc(hT_ready, 1)

            def kk(G):
                pe.wait_ge(xk_split, KC * (G + 1))
                for h in range(KC):
                    project(bank_g[h][:], ffn_hi[:, 0], ffn_lo[:, 0], slice(h * P, (h + 1) * P),
                            mix_hi[:, 0:KC], mix_lo[:, 0:KC]).then_inc(k_ready, 1)

            def by_rows(banks, x_hi, x_lo, w_hi, w_lo, done):
                for i in range(2):
                    for t in range(2 * i, 2 * i + 2):
                        rows = slice(t * P, (t + 1) * P)
                        last = product(banks[i][:, (t % 2) * C:(t % 2 + 1) * C],
                                       [(x_hi[:, k, rows], x_lo[:, k, rows], w_hi[:, k, :], w_lo[:, k, :]) for k in range(KC)])
                    last.then_inc(done, 1)

            def rr(G):
                pe.wait_ge(xr_split, KC * (G + 1))
                if G + 1 == NG:
                    pe.wait_ge(o_added, FIRST[NG])
                by_rows(bank_o, mix_hi[:, KC:], mix_lo[:, KC:], ffn_hi[:, 1], ffn_lo[:, 1], r_ready)

            def ff(G):
                pe.wait_ge(act_split, KC * (G + 1))
                by_rows(bank_g, act_hi, act_lo, ffn_hi[:, 2], ffn_lo[:, 2], ff_ready)

            def scores(G, i):
                c, p = STEPS[G][i]
                s, rows = FIRST[G] + i, slice(p * P, (p + 1) * P)
                keys = slice(c * GW, c * GW + max(width(G, c, p), 2 * P))
                if i >= 2:
                    pe.wait_ge(s_used, s - 1)
                else:
                    pe.wait_ge(kT_split, KC * (G + 1))
                product(bank_s[s % 2][:, 0:keys.stop - keys.start],
                        [(xT_hi[:, k, rows], xT_lo[:, k, rows], kT_hi[:, k, keys], kT_lo[:, k, keys]) for k in range(KC)])\
                    .then_inc(s_ready, 1)

            def pT(G, i):
                s = FIRST[G] + i
                pe.wait_ge(exp_done, s + 1)
                if i == 0:
                    pe.wait_ge(e_copied, G + 1)
                for b in range(width(G, *STEPS[G][i]) // P):
                    last = nc.tensor.transpose(bank_p[s % 2][:, b * P:(b + 1) * P], prob[:, s % 2, b * P:(b + 1) * P], ident[:])
                last.then_inc(pT_ready, 1)

            def pv(G, i):
                c, p = STEPS[G][i]
                s = FIRST[G] + i
                pe.wait_ge(pT_split, s + 1)
                if i >= 2:
                    pe.wait_ge(o_added, s - 1)
                elif G > 0:
                    pe.wait_ge(gate_ready, 2 * G)
                product(bank_o[s % 2][:, 0:C],
                        [(pT_hi[:, s % 2, b * P:(b + 1) * P], pT_lo[:, s % 2, b * P:(b + 1) * P],
                          v_hi[:, c * TG + b, :], v_lo[:, c * TG + b, :]) for b in range(width(G, c, p) // P)])\
                    .then_inc(o_ready, 1)

            pe.wait_ge(const_ready, 3)
            for i, (raw, bank, need) in enumerate(((raw_k, bank_g[0], 32), (raw_q, bank_g[1], 32), (raw_v, bank_s[0], 80))):
                pe.wait_ge(w_loaded, need if i else 80)
                for d in range(KC):
                    for k in range(KC):
                        last = nc.tensor.transpose(bank[:, d * C + k * P:d * C + (k + 1) * P], raw[:, k, d * P:(d + 1) * P], ident[:])
                last.then_inc(fold_ready, 1)
            pe.wait_ge(fold_moved, 3)
            xT(0)
            for h in range(KC):
                for d in range(KC):
                    last = mm(bank_s[1][:, h * C:(h + 1) * C], wkT[:, d, h * P:(h + 1) * P], wqT[:, d, :], start=d == 0, stop=d == KC - 1)
            last.then_inc(fold_ready, 1)
            for h in range(KC):
                for d in range(KC):
                    last = mm(bank_o[h][:, 0:C], wvT[:, d, h * P:(h + 1) * P], raw_o[:, d, :], start=d == 0, stop=d == KC - 1)
            last.then_inc(fold_ready, 1)
            pe.wait_ge(col_loaded, 80)
            for dst, left, vec in ((0, wkT, BQ), (KC, wqT, BK)):
                for h in range(KC):
                    for d in range(KC):
                        last = mm(bank_p[0][:, dst + h:dst + h + 1], left[:, d, h * P:(h + 1) * P], cols[:, vec, d:d + 1],
                                  start=d == 0, stop=d == KC - 1)
            for d in range(KC):
                last = mm(bank_p[0][:, 2 * KC:2 * KC + 1], cols[:, BK, d:d + 1].to_broadcast([P, P]), cols[:, BQ, d:d + 1],
                          start=d == 0, stop=d == KC - 1)
            last.then_inc(fold_ready, 1)
            for d in range(KC):
                last = mm(bank_p[1][:, 0:C], cols[:, BV, d:d + 1].to_broadcast([P, P]), raw_o[:, d, :], start=d == 0, stop=d == KC - 1)
            last.then_inc(fold_ready, 1)
            pe.wait_ge(fold_split, 1)
            kT(0)
            pe.wait_ge(fold_split, 3)
            pe.wait_ge(bias_ready, 1)
            vv(0)
            e(0)
            scores(0, 0)
            scores(0, 1)
            pe.wait_ge(ffn_loaded, 48)
            for i in range(3):
                if i == 2:
                    pe.wait_ge(ffn_split, 1)
                for k in range(KC):
                    for d in range(KC):
                        last = nc.tensor.transpose(ffn_bank[i][:, k * C + d * P:k * C + (d + 1) * P],
                                                   raw_ffn[:, i, d, k * P:(k + 1) * P], ident[:])
                last.then_inc(ffn_ready, 1)
            pe.wait_ge(ffn_split, 3)

            for G in range(NG):
                n = len(STEPS[G])
                for i in range(n + 2):
                    if 2 <= i < n:
                        scores(G, i)
                    if i == n and G + 1 < NG:
                        xT(G + 1)
                    if 1 <= i <= n:
                        pT(G, i - 1)
                    if i == 1 and G > 0:
                        ff(G - 1)
                    if i >= 2:
                        pv(G, i - 2)
                if G + 1 < NG:
                    kT(G + 1)
                    vv(G + 1)
                hTr(G)
                if G + 1 < NG:
                    e(G + 1)
                    scores(G + 1, 0)
                    scores(G + 1, 1)
                kk(G)
                rr(G)
            ff(NG - 1)


_INS = ["L0_attn_y_all", "L0_attn_Wq", "L0_attn_bq", "L0_attn_Wk", "L0_attn_bk", "L0_attn_Wv", "L0_attn_bv", "L0_attn_Wo",
        "L0_attn_bo", "L0_ffn_W_r", "L0_ffn_W_k", "L0_ffn_W_v", "L0_ffn_mu_r", "L0_ffn_mu_k"]


def kernel(**inputs):
    import numpy as _np
    import concourse.bacc as _bacc
    from concourse import mybir as _mybir
    from concourse.bass_utils import run_bass_kernel_spmd as _run

    nc = _bacc.Bacc("TRN2", target_bir_lowering=False, num_devices=1)
    arrays, args = {}, []
    for name in _INS:
        a = _np.ascontiguousarray(inputs[name])
        arrays[f"in_{name}_dram"] = a
        args.append(nc.dram_tensor(f"in_{name}_dram", a.shape, _mybir.dt.from_np(a.dtype), kind="ExternalInput").ap())
    shape = arrays["in_L0_attn_y_all_dram"].shape
    args.append(nc.dram_tensor("out_0_dram", shape, _mybir.dt.float32, kind="ExternalOutput").ap())
    attention_channel_mix_block(nc, *args)
    r = _run(nc, [arrays], core_ids=[0])
    return r.results[0]["out_0_dram"]
```

```python
import concourse.bass as bass
from concourse import mybir
from contextlib import ExitStack


def attention_channel_mix_block(nc, y, wq, bq, wk, bk, wv, bv, wo, bo, w_r, w_k, w_v, mu_r, mu_k, out):
    f32, f32r, bf16 = mybir.dt.float32, mybir.dt.float32r, mybir.dt.bfloat16
    ALU, ACT = mybir.AluOpType, mybir.ActivationFunctionType

    B, T, C = y.shape
    P = 128
    KC = C // P
    TG = 4
    GW = TG * P
    GB = T // GW
    NG = B * GB
    NX = 4
    NT = 2
    SCALE = float(C) ** -0.5
    MASKED = 1.0e30
    LARGEST = 3.0e38
    FFN_SCALE = (1.0, 1.0, 0.5)
    EPS = 1e-5

    STEPS = [(G, c, p) for G in range(NG - 1) for c in range(G % GB + 1) for p in range(TG)]
    STEPS += [(NG - 1, c, p) for p0 in range(0, TG, 2) for c in range(GB) for p in (p0, p0 + 1)]
    NS = len(STEPS)
    FIRST = [sum(TG * (g % GB + 1) for g in range(G)) for G in range(NG + 1)]

    def diagonal(s):
        return 0 <= s < NS and STEPS[s][1] == STEPS[s][0] % GB

    def width(s):
        return (STEPS[s][2] + 1) * P if diagonal(s) else GW

    def chunk_free(G):
        g = G % GB
        return FIRST[G - g - 1] + TG * (g + 1)

    JOBS = [(G, 0, TG) for G in range(NG - 1)] + [(NG - 1, 0, TG // 2), (NG - 1, TG // 2, TG // 2)]
    LAST = len(JOBS) - 1

    def span(J):
        return slice(JOBS[J][1] * P, (JOBS[J][1] + JOBS[J][2]) * P)

    def pair(J, i):
        return (JOBS[J][0] * TG + JOBS[J][1]) // 2 + i

    STATS_AT = {2: (2, 2), 3: (12, 14), 4: (18, 22), 5: (31, 34), 6: (41, 41), 7: (53, 54)}
    APPLY_AT = {1: (-2, -2), 2: (3, 4), 3: (15, 15), 4: (25, 25), 5: (35, 36), 6: (45, 45), 7: (56, 57)}
    XT_AT = {1: (-1, -1), 2: (5, 5), 3: (17, 18), 4: (28, 29), 5: (38, 39), 6: (46, 47), 7: (58, 60)}
    KT_AT = {1: (1, 1), 2: (8, 9), 3: (22, 22), 4: (31, 35), 5: (40, 43), 6: (52, 53), 7: (62, 63)}
    V_AT = {1: (2, 4), 2: (8, 9), 3: (26, 28), 4: (37, 37), 5: (44, 44), 6: (56, 59), 7: (63, 64)}
    DOT_AT = {1: (0, 1), 2: (11, 12), 3: (19, 21), 4: (31, 33), 5: (42, 43), 6: (54, 55), 7: (64, 64)}
    E_AT = {1: (4,), 2: (14,), 3: (24,), 4: (36,), 5: (45,), 6: (56,), 7: (66,)}
    HT_AT = [(6, 7), (14, 15), (26, 27), (41, 42), (49, 50), (61, 62), (67, 68), (76, 76), (NS + 1, NS + 2)]
    MIX_AT = [(8, 9), (16, 17), (28, 30), (43, 44), (50, 52), (62, 63), (68, 69), (76, 77), (NS + 3, NS + 3)]
    KK_AT = [(11, 11), (19, 20), (31, 32), (46, 46), (54, 55), (65, 66), (73, 75), (79, NS), (NS + 4, NS + 4)]
    RR_AT = [(12, 13), (21, 21), (33, 34), (48, 48), (56, 56), (67, 68), (74, 77), (NS,), (NS + 4,)]
    FF_AT = [(16, 16), (25, 27), (34, 34), (49, 51), (59, 60), (71, 72), (77, 78), (NS + 1,), (NS + 4,)]
    END = NS + 6

    def stages(s):
        found = []
        for name, table in (("mix", MIX_AT), ("apply", APPLY_AT), ("dot", DOT_AT), ("stats", STATS_AT), ("hT", HT_AT), ("kk", KK_AT),
                            ("rr", RR_AT), ("ff", FF_AT), ("xT", XT_AT), ("kT", KT_AT), ("v", V_AT), ("e", E_AT)):
            for n, at in (table.items() if isinstance(table, dict) else enumerate(table)):
                for i in range(len(at)):
                    if at[i] == s:
                        finer = name in ("mix", "dot", "stats", "apply")
                        found += [(name, n, u) for u in ((2 * i, 2 * i + 1) if finer else (i,))]
        return found

    SLOTS = range(-2, END)
    STAGES = {s: stages(s) for s in SLOTS}

    ON_PE = ("xT", "kT", "v", "e", "hT", "kk", "rr", "ff")
    USES = [("xT", 0, 0), ("xT", 0, 1), ("kT", 0, 0), ("kT", 0, 1), ("v", 0, 0), ("v", 0, 1), ("e", 0, 0)]
    USES += [u for s in SLOTS for u in STAGES[s] if u[0] in ON_PE]

    y_t = y.rearrange("b (n p) c -> p (b n) c", p=P)
    out_t = out.rearrange("b (n p) c -> p (b n) c", p=P)

    ctx = ExitStack()
    with ctx:
        def sb(name, shape, dt=f32):
            return ctx.enter_context(nc.sbuf_tensor(name, shape, dt))

        def sem(name):
            return ctx.enter_context(nc.semaphore(name))

        x_in = sb("x_in", [P, NX, TG, C])
        xhat = sb("xhat", [P, TG, C])
        o_sum = sb("o_sum", [P, TG, C])
        h_row = sb("h_row", [P, TG, C])
        gate = sb("gate", [P, TG, C])
        xT_hi, xT_lo = sb("xT_hi", [P, NT, KC, GW], f32r), sb("xT_lo", [P, NT, KC, GW], f32r)
        kT_hi, kT_lo = sb("kT_hi", [P, KC, T], f32r), sb("kT_lo", [P, KC, T], f32r)
        v_hi, v_lo = sb("v_hi", [P, T // P, C], f32r), sb("v_lo", [P, T // P, C], f32r)
        e_row = sb("e_row", [P, T])
        prob = sb("prob", [P, 2, GW])
        pT_hi, pT_lo = sb("pT_hi", [P, 2, GW], f32r), sb("pT_lo", [P, 2, GW], f32r)
        hT = sb("hT", [P, KC, GW + 1])
        mix = sb("mix", [P, 2 * KC, GW])
        mix_hi, mix_lo = sb("mix_hi", [P, 2 * KC, GW], f32r), sb("mix_lo", [P, 2 * KC, GW], f32r)
        act_hi, act_lo = sb("act_hi", [P, KC, GW], f32r), sb("act_lo", [P, KC, GW], f32r)
        act = mix[:, 0:KC, :]
        wkq_hi, wkq_lo = sb("wkq_hi", [P, KC, C], f32r), sb("wkq_lo", [P, KC, C], f32r)
        wvo_hi, wvo_lo = sb("wvo_hi", [P, KC, C], f32r), sb("wvo_lo", [P, KC, C], f32r)
        we_row = sb("we_row", [P, C])
        ffn_hi, ffn_lo = sb("ffn_hi", [P, 3, KC, C], f32r), sb("ffn_lo", [P, 3, KC, C], f32r)
        cols = sb("cols", [P, 7, KC])
        BQ, BK, BV, MU_R, MU_K, OM_R, OM_K = range(7)
        bkq = sb("bkq", [P, KC])
        e_const = sb("e_const", [P, 1])
        e_col = sb("e_col", [P, TG])
        scratch = sb("scratch", [P, C])
        b_out = sb("b_out", [P, C])
        ident = sb("ident", [P, P])
        ident_b, mask_b = sb("ident_b", [P, P], bf16), sb("mask_b", [P, P], bf16)
        minus_half = sb("minus_half", [P, TG])
        stats = sb("stats", [P, TG, 6])
        mean_var = sb("mean_var", [P, TG, 2])
        var_eps = sb("var_eps", [P, TG])
        rstd = sb("rstd", [P, TG])
        stats2 = sb("stats2", [P, TG, 6])
        mean_var2 = sb("mean_var2", [P, TG, 2])
        var_eps2 = sb("var_eps2", [P, TG])
        rstd2 = sb("rstd2", [P, TG])
        neg_max = sb("neg_max", [P, 2, TG])
        alpha = sb("alpha", [P, 2, TG])
        row_sum = sb("row_sum", [P, TG])
        part_sum = sb("part_sum", [P, 2, TG])
        inv_sum = sb("inv_sum", [P, TG])
        raw_k, raw_q = h_row[:, 0:2, :], h_row[:, 2:4, :]
        raw_v, raw_o = o_sum[:, 0:2, :], o_sum[:, 2:4, :]
        raw_ffn = mix[:, 0:3, :].rearrange("p m (k c) -> p m k c", k=KC)
        wkT, wqT = [prob[:, i, :].rearrange("p (k c) -> p k c", k=KC) for i in range(2)]
        wvT = hT[:, 0, 0:GW].rearrange("p (k c) -> p k c", k=KC)
        bo_rows = gate[:, 0, :]
        mask_f = gate[:, 1, 0:P]

        bank_s, bank_p, bank_o, bank_g = [
            [ctx.enter_context(nc.psum_tensor(f"{n}{i}", [P, GW], f32)) for i in range(2)] for n in ("S", "PT", "O", "G")]
        ffn_bank = (bank_s[0], bank_s[1], bank_o[1])

        def bank_of(*use):
            return bank_g[USES.index(use) % 2]

        x_loaded = [sem(f"x_loaded{i}") for i in range(NX)]
        (wk_loaded, wq_loaded, wv_loaded, wo_loaded, bo_loaded, col_loaded, ffn_loaded, stored, const_ready, fold_ready, fold_moved, fold_split,
         bias_ready, ffn_ready, ffn_high, ffn_split, om_ready, row_ready, stat1, var1_ready, eps1_ready, rstd1_ready, xhat_ready, xb_ready,
         xT_ready, xT_high, xT_split, kT_ready, kT_high, kT_split, v_ready, v_high, v_split, dotted,
         e_ready, e_copied, s_ready, s_used, exp_done, pT_ready, pT_high,
         pT_split, sum_done, inv_ready, o_ready, o_added, x1_ready, stat2, var2_ready, eps2_ready, rstd2_ready,
         h_ready, hT_ready, mu_done, prev_ready, mixed, mix_high, mix_split, k_ready, k_relu,
         squared, act_high, act_split, r_ready, gate_ready, ff_ready, ff_used, out_ready, last_ff_ready, last_gated, last_out_ready) = [sem(n) for n in (
            "wk_loaded wq_loaded wv_loaded wo_loaded bo_loaded col_loaded ffn_loaded stored const_ready fold_ready fold_moved fold_split "
            "bias_ready ffn_ready ffn_high ffn_split om_ready row_ready stat1 var1_ready eps1_ready rstd1_ready xhat_ready xb_ready "
            "xT_ready xT_high xT_split kT_ready kT_high kT_split v_ready v_high v_split dotted "
            "e_ready e_copied s_ready s_used exp_done pT_ready pT_high "
            "pT_split sum_done inv_ready o_ready o_added x1_ready stat2 var2_ready eps2_ready rstd2_ready "
            "h_ready hT_ready mu_done prev_ready mixed mix_high mix_split k_ready k_relu "
            "squared act_high act_split r_ready gate_ready ff_ready ff_used out_ready last_ff_ready last_gated last_out_ready").split()]

        block = ctx.enter_context(nc.Block())

        def halves(w):
            return w.rearrange("(k p) c -> p k c", p=P)

        @block.sync
        def _(sp):
            def load(G):
                sp.dma_start(x_in[:, G % NX], y_t[:, G * TG:(G + 1) * TG, :]).then_inc(x_loaded[G % NX], 16)

            sp.dma_start(raw_k, halves(wk)).then_inc(wk_loaded, 16)
            sp.dma_start(raw_q, halves(wq)).then_inc(wq_loaded, 16)
            load(0)
            sp.dma_start(raw_v, halves(wv)).then_inc(wv_loaded, 16)
            sp.dma_start(raw_o, halves(wo)).then_inc(wo_loaded, 16)
            with nc.allow_non_contiguous_dma(reason="vectors of 256 numbers, once"):
                for i, vec in enumerate((bq, bk, bv, mu_r, mu_k)):
                    sp.dma_start(cols[:, i, :], vec.rearrange("(k p) -> p k", p=P)).then_inc(col_loaded, 16)
            sp.dma_start(bo_rows, bo.rearrange("(a c) -> a c", a=1).to_broadcast([P, C])).then_inc(bo_loaded, 16)
            for i, w in enumerate((w_k, w_r, w_v)):
                sp.dma_start(raw_ffn[:, i], halves(w)).then_inc(ffn_loaded, 16)
            load(1)
            for G in range(2, NX):
                load(G)
            for G in range(NG):
                for i in range(2):
                    if (G, i) == (NG - 1, 1):
                        break
                    sp.wait_ge(out_ready, 2 * G + i + 1)
                    if i == 1 and G + NX < NG:
                        load(G + NX)
                    t = G * TG + 2 * i
                    sp.dma_start(out_t[:, t:t + 2, :], gate[:, 2 * i:2 * i + 2, :]).then_inc(stored, 16)
            for i in range(TG // 2):
                sp.wait_ge(last_out_ready, i + 1)
                t = NG * TG - TG // 2 + i
                sp.dma_start(out_t[:, t, :], gate[:, TG // 2 + i, :]).then_inc(stored, 16)
            sp.wait_ge(stored, 16 * (2 * NG + 1))

        @block.gpsimd
        def _(pool):
            g = nc.gpsimd
            g.memset(ident[:], 0.0).then_inc(const_ready, 1)
            g.memset(minus_half[:], -0.5).then_inc(const_ready, 1)
            g.memset(mask_f, 0.0).then_inc(const_ready, 1)
            pool.wait_ge(const_ready, 3)
            g.affine_select(out=ident[:], in_=ident[:], compare_op=ALU.not_equal, fill=1.0, base=0,
                            pattern=[[-1, P]], channel_multiplier=1).then_inc(const_ready, 1)
            g.affine_select(out=mask_f, in_=mask_f, compare_op=ALU.is_ge, fill=MASKED, base=0,
                            pattern=[[-1, P]], channel_multiplier=1).then_inc(const_ready, 1)
            pool.wait_ge(const_ready, 5)
            g.tensor_copy(ident_b[:], ident[:]).then_inc(const_ready, 1)
            g.tensor_copy(mask_b[:], mask_f).then_inc(const_ready, 1)

            def rsqrt(mv, ve, rs, ready, eps_done, done, count, tiles):
                pool.wait_ge(ready, count)
                g.tensor_scalar(ve[:, tiles], mv[:, tiles, 1], EPS, None, ALU.add).then_inc(eps_done, 1)
                pool.wait_ge(eps_done, count)
                g.tensor_tensor(rs[:, tiles], ve[:, tiles], minus_half[:, tiles], ALU.pow).then_inc(done, 1)

            def rsqrt1(G):
                rsqrt(mean_var, var_eps, rstd, var1_ready, eps1_ready, rstd1_ready, G + 1, slice(0, TG))

            def rsqrt2(G, p):
                rsqrt(mean_var2, var_eps2, rstd2, var2_ready, eps2_ready, rstd2_ready, TG * G + p + 1, slice(p, p + 1))

            def add_bias(G, i):
                pool.wait_ge(xhat_ready, TG * G + 2 * i + 2)
                if G == 0 and i == 0:
                    pool.wait_ge(bias_ready, 1)
                for t in range(2 * i, 2 * i + 2):
                    last = g.tensor_tensor(x_in[:, G % NX, t, :], x_in[:, G % NX, t, :], b_out[:], ALU.add)
                last.then_inc(xb_ready, 1)

            def mix_low(J, j):
                r = span(J)
                pool.wait_ge(mix_high, 2 * KC * J + j + 1)
                g.tensor_tensor(mix_lo[:, j, r], mix[:, j, r], mix_hi[:, j, r].bitcast(f32), ALU.subtract).then_inc(mix_split, 1)

            def act_low(J, h):
                r = span(J)
                pool.wait_ge(act_high, KC * J + h + 1)
                g.tensor_tensor(act_lo[:, h, r], act[:, h, r], act_hi[:, h, r].bitcast(f32), ALU.subtract).then_inc(act_split, 1)

            def add_x1(J, i):
                pool.wait_ge(ff_used, pair(J, i) + 1)
                t = JOBS[J][1] + 2 * i
                g.tensor_tensor(gate[:, t:t + 2, :], gate[:, t:t + 2, :], x_in[:, JOBS[J][0] % NX, t:t + 2, :], ALU.add)\
                    .then_inc(out_ready, 1)

            rsqrt1(0)
            rsqrt1(1)
            add_bias(0, 0)
            add_bias(0, 1)
            for s in SLOTS:
                if diagonal(s - 1):
                    rsqrt2(STEPS[s - 1][0], STEPS[s - 1][2])
                for stage, n, i in STAGES.get(s - 1, ()):
                    if stage == "mix" and n < LAST:
                        mix_low(n, i)
                for stage, n, i in STAGES[s]:
                    if stage == "stats" and i == TG - 1:
                        rsqrt1(n)
                    elif stage == "apply" and i % 2:
                        add_bias(n, i // 2)
                    elif stage == "kk" and n < LAST:
                        act_low(n, i)
                    elif stage == "ff" and n < LAST:
                        add_x1(n, i)

        @block.scalar
        def _(sc):
            a = nc.scalar

            def high(dst, src, done, **kw):
                a.activation(dst, src, ACT.Copy, **kw).then_inc(done, 1)

            def pairs(bank):
                return bank[:].rearrange("p (t c) -> p t c", c=C)

            def xT_part(G, h):
                sc.wait_ge(xT_ready, KC * G + h + 1)
                if G >= NT and h == 0:
                    sc.wait_ge(s_ready, FIRST[G - NT + 1])
                high(xT_hi[:, G % NT, h], bank_of("xT", G, h)[:], xT_high)

            def kT_part(G, h):
                sc.wait_ge(kT_ready, KC * G + h + 1)
                if G == 0 and h == 0:
                    sc.wait_ge(fold_split, 3)
                if G >= GB and h == 0:
                    sc.wait_ge(s_ready, chunk_free(G))
                g0 = (G % GB) * GW
                a.activation(kT_hi[:, h, g0:g0 + GW], bank_of("kT", G, h)[:], ACT.Identity, bias=bkq[:, h:h + 1])\
                    .then_inc(kT_high, 1)

            def v_part(G, i):
                sc.wait_ge(v_ready, 2 * G + i + 1)
                if G >= GB and i == 0:
                    sc.wait_ge(o_ready, chunk_free(G))
                t = (G % GB) * TG + 2 * i
                high(v_hi[:, t:t + 2, :], pairs(bank_of("v", G, i)), v_high)

            def e_part(G):
                sc.wait_ge(e_ready, G + 1)
                if G >= GB:
                    sc.wait_ge(s_used, chunk_free(G))
                g0 = (G % GB) * GW
                a.activation(e_row[:, g0:g0 + GW], bank_of("e", G, 0)[:], ACT.Identity, bias=e_const[:, 0:1]).then_inc(e_copied, 1)

            def exps(s):
                G, c, p = STEPS[s]
                w = width(s)
                sc.wait_ge(s_used, s + 1)
                total = row_sum[:, p:p + 1] if c == 0 else part_sum[:, c % 2, p:p + 1]
                if c > 0:
                    a.activation(alpha[:, c % 2, p:p + 1], neg_max[:, (c - 1) % 2, p:p + 1], ACT.Exp,
                                 bias=neg_max[:, c % 2, p:p + 1], scale=-1.0)
                a.activation(prob[:, s % 2, 0:w], prob[:, s % 2, 0:w], ACT.Exp, bias=neg_max[:, c % 2, p:p + 1], scale=-1.0,
                             accum_out=total).then_inc(exp_done, 1)

            def pT_part(s):
                w = width(s)
                sc.wait_ge(pT_ready, s + 1)
                high(pT_hi[:, s % 2, 0:w], bank_p[s % 2][:, 0:w], pT_high)

            def hT_part(J, h):
                G, r = JOBS[J][0], span(J)
                sc.wait_ge(hT_ready, KC * J + h + 1)
                if J > 0 and h == 0:
                    sc.wait_ge(prev_ready, G + 1)
                    sc.wait_ge(act_split, KC * J)
                bank = bank_of("hT", J, h)
                a.activation(hT[:, h, r.start + 1:r.stop + 1], bank[:, r], ACT.Copy)
                for j, mu in ((h, MU_K), (KC + h, MU_R)):
                    last = a.activation(mix[:, j, r], bank[:, r], ACT.Copy, scale=cols[:, mu, h:h + 1])
                last.then_inc(mu_done, 1)

            def mix_part(J, j):
                r = span(J)
                sc.wait_ge(mixed, 2 * KC * J + j + 1)
                high(mix_hi[:, j, r], mix[:, j, r], mix_high)

            def kk_part(J, h):
                n, r = KC * J + h + 1, span(J)
                sc.wait_ge(k_ready, n)
                a.activation(act[:, h, r], bank_of("kk", J, h)[:, r], ACT.Relu).then_inc(k_relu, 1)
                sc.wait_ge(k_relu, n)
                a.activation(act[:, h, r], act[:, h, r], ACT.Square).then_inc(squared, 1)
                sc.wait_ge(squared, n)
                high(act_hi[:, h, r], act[:, h, r], act_high)

            def rr_part(J, i):
                t = JOBS[J][1] + 2 * i
                sc.wait_ge(r_ready, pair(J, i) + 1)
                if J > 0:
                    sc.wait_ge(stored, 32 * JOBS[J][0])
                a.activation(gate[:, t:t + 2, :], pairs(bank_of("rr", J, i)), ACT.Tanh, scale=0.5).then_inc(gate_ready, 1)

            def ffn_part(i):
                sc.wait_ge(ffn_ready, i + 1)
                high(ffn_hi[:, i], pairs(ffn_bank[i]), ffn_high, scale=FFN_SCALE[i])

            sc.wait_ge(fold_ready, 1)
            high(wkT, pairs(bank_p[0]), fold_moved)
            sc.wait_ge(fold_ready, 2)
            high(wqT, pairs(bank_p[1]), fold_moved)
            sc.wait_ge(fold_ready, 3)
            high(wkq_hi[:], pairs(bank_s[1]), fold_moved, scale=-SCALE)
            sc.wait_ge(fold_ready, 4)
            high(wvT, pairs(bank_s[0]), fold_moved)
            for h in range(KC):
                xT_part(0, h)
            sc.wait_ge(fold_ready, 5)
            for h in range(KC):
                high(wvo_hi[:, h, :], bank_o[h][:, 0:C], fold_moved)
            ffn_part(0)
            ffn_part(1)
            for h in range(KC):
                kT_part(0, h)
            for i in range(2):
                v_part(0, i)
            ffn_part(2)
            e_part(0)

            for s in SLOTS:
                if 0 <= s + 1 < NS:
                    pT_part(s + 1)
                if s + 2 < NS:
                    exps(s + 2)
                for stage, n, i in STAGES.get(s - 1, ()):
                    if stage == "mix":
                        mix_part(n, i)
                for stage, n, i in STAGES[s]:
                    if stage == "xT":
                        xT_part(n, i)
                    elif stage == "kT":
                        kT_part(n, i)
                    elif stage == "v":
                        v_part(n, i)
                    elif stage == "e":
                        e_part(n)
                    elif stage == "hT":
                        hT_part(n, i)
                    elif stage == "kk":
                        kk_part(n, i)
                    elif stage == "rr":
                        rr_part(n, i)

        @block.vector
        def _(dve):
            v = nc.vector

            def low(dst, src, hi, done):
                v.tensor_tensor(dst, src, hi.bitcast(f32), ALU.subtract).then_inc(done, 1)

            def ln1_stats(G, t):
                if t == 0:
                    dve.wait_ge(x_loaded[G % NX], 16 * (G // NX + 1))
                v.bn_stats(stats[:, t, :], x_in[:, G % NX, t, :]).then_inc(stat1, 1)
                if t == TG - 1:
                    dve.wait_ge(stat1, TG * (G + 1))
                    for u in range(TG):
                        last = v.bn_aggr(mean_var[:, u, :], stats[:, u, :])
                    last.then_inc(var1_ready, 1)

            def ln1_apply(G, t):
                if t == 0:
                    dve.wait_ge(rstd1_ready, G + 1)
                    if G > 0:
                        dve.wait_ge(xT_ready, KC * G)
                        dve.wait_ge(dotted, TG * G)
                v.tensor_scalar(xhat[:, t, :], x_in[:, G % NX, t, :], mean_var[:, t, 0:1], rstd[:, t:t + 1],
                                ALU.subtract, ALU.mult).then_inc(xhat_ready, 1)

            def xT_part(G, h):
                dve.wait_ge(xT_high, KC * G + h + 1)
                low(xT_lo[:, G % NT, h], bank_of("xT", G, h)[:], xT_hi[:, G % NT, h], xT_split)

            def kT_part(G, h):
                dve.wait_ge(kT_high, KC * G + h + 1)
                g0 = (G % GB) * GW
                v.scalar_tensor_tensor(kT_lo[:, h, g0:g0 + GW], bank_of("kT", G, h)[:], bkq[:, h:h + 1],
                                       kT_hi[:, h, g0:g0 + GW].bitcast(f32), ALU.add, ALU.subtract).then_inc(kT_split, 1)

            def v_part(G, i):
                dve.wait_ge(v_high, 2 * G + i + 1)
                t = (G % GB) * TG + 2 * i
                low(v_lo[:, t:t + 2, :], bank_of("v", G, i)[:].rearrange("p (t c) -> p t c", c=C), v_hi[:, t:t + 2, :], v_split)

            def e_dot(G, t):
                if t == 0:
                    dve.wait_ge(row_ready, 1)
                    dve.wait_ge(xhat_ready, TG * (G + 1))
                    if G > 0:
                        dve.wait_ge(e_ready, G)
                if G + t > 0:
                    dve.wait_ge(dotted, TG * G + t)
                v.tensor_tensor_reduce(out=scratch[:], in0=xhat[:, t, :], in1=we_row[:], scale=1.0, scalar=0.0,
                                       op0=ALU.mult, op1=ALU.add, accum_out=e_col[:, t:t + 1]).then_inc(dotted, 1)

            def ffn_low(i):
                dve.wait_ge(ffn_high, i + 1)
                v.scalar_tensor_tensor(ffn_lo[:, i], ffn_bank[i][:].rearrange("p (k c) -> p k c", k=KC), FFN_SCALE[i],
                                       ffn_hi[:, i].bitcast(f32), ALU.mult, ALU.subtract).then_inc(ffn_split, 1)

            for t in range(TG):
                ln1_stats(0, t)
            for t in range(TG):
                ln1_apply(0, t)
            dve.wait_ge(col_loaded, 80)
            v.tensor_scalar(cols[:, OM_R:OM_K + 1, :], cols[:, MU_R:MU_K + 1, :], -1.0, 1.0, ALU.mult, ALU.add)\
                .then_inc(om_ready, 1)
            dve.wait_ge(fold_moved, 3)
            v.scalar_tensor_tensor(wkq_lo[:], bank_s[1][:].rearrange("p (k c) -> p k c", k=KC), -SCALE,
                                   wkq_hi[:].bitcast(f32), ALU.mult, ALU.subtract).then_inc(fold_split, 1)
            for h in range(KC):
                xT_part(0, h)
            dve.wait_ge(fold_moved, 6)
            for h in range(KC):
                last = v.tensor_tensor(wvo_lo[:, h, :], bank_o[h][:, 0:C], wvo_hi[:, h, :].bitcast(f32), ALU.subtract)
            last.then_inc(fold_split, 1)
            ffn_low(0)
            ffn_low(1)
            dve.wait_ge(fold_ready, 6)
            v.tensor_scalar(e_const[:], bank_p[0][:, KC:KC + 1], -SCALE, None, ALU.mult)
            v.tensor_scalar(we_row[:], bank_p[0][:, C:2 * C], -SCALE, None, ALU.mult).then_inc(row_ready, 1)
            v.tensor_scalar(bkq[:], bank_p[0][:, 0:KC], -SCALE, None, ALU.mult).then_inc(fold_split, 1)
            dve.wait_ge(bo_loaded, 16)
            dve.wait_ge(fold_ready, 7)
            v.tensor_tensor(b_out[:], bank_p[1][:, 0:C], bo_rows, ALU.add).then_inc(bias_ready, 1)
            for t in range(TG):
                ln1_stats(1, t)
            for h in range(KC):
                kT_part(0, h)
            for t in range(TG):
                e_dot(0, t)
            for i in range(2):
                v_part(0, i)
            ffn_low(2)
            v.memset(hT[:, :, 0:1], 0.0).then_inc(prev_ready, 1)

            def scores(s):
                G, c, p = STEPS[s]
                w = width(s)
                if diagonal(s) and p == 0:
                    dve.wait_ge(e_copied, G + 1)
                dve.wait_ge(s_ready, s + 1)
                before = LARGEST if c == 0 else neg_max[:, (c - 1) % 2, p:p + 1]
                v.tensor_tensor_reduce(out=prob[:, s % 2, 0:w], in0=bank_s[s % 2][:, 0:w], in1=e_row[:, c * GW:c * GW + w],
                                       scale=1.0, scalar=before, op0=ALU.add, op1=ALU.min,
                                       accum_out=neg_max[:, c % 2, p:p + 1]).then_inc(s_used, 1)

            def pT_part(s):
                G, c, p = STEPS[s]
                w = width(s)
                dve.wait_ge(pT_high, s + 1)
                low(pT_lo[:, s % 2, 0:w], bank_p[s % 2][:, 0:w], pT_hi[:, s % 2, 0:w], pT_split)
                if c > 0:
                    v.scalar_tensor_tensor(row_sum[:, p:p + 1], row_sum[:, p:p + 1], alpha[:, c % 2, p:p + 1],
                                           part_sum[:, c % 2, p:p + 1], ALU.mult, ALU.add).then_inc(sum_done, 1)

            def add_x(s, o, done):
                G, c, p = STEPS[s]
                v.reciprocal(inv_sum[:, p:p + 1], row_sum[:, p:p + 1]).then_inc(inv_ready, 1)
                dve.wait_ge(inv_ready, TG * G + p + 1)
                dve.wait_ge(xb_ready, 2 * G + p // 2 + 1)
                x1 = x_in[:, G % NX, p, :]
                v.scalar_tensor_tensor(x1, o, inv_sum[:, p:p + 1], x1, ALU.mult, ALU.add).then_inc(done, 1)

            def o_part(s):
                G, c, p = STEPS[s]
                o = bank_o[s % 2][:, 0:C]
                dve.wait_ge(o_ready, s + 1)
                if diagonal(s) and c == 0:
                    add_x(s, o, o_added)
                elif c == 0:
                    v.tensor_copy(o_sum[:, p, :], o).then_inc(o_added, 1)
                else:
                    v.scalar_tensor_tensor(o_sum[:, p, :], o_sum[:, p, :], alpha[:, c % 2, p:p + 1], o,
                                           ALU.mult, ALU.add).then_inc(o_added, 1)

            def x1_part(s):
                G, c, p = STEPS[s]
                n = TG * G + p + 1
                x1 = x_in[:, G % NX, p, :]
                dve.wait_ge(o_added, s + 1)
                if c > 0:
                    dve.wait_ge(sum_done, sum(step[1] > 0 for step in STEPS[:s + 1]))
                    add_x(s, o_sum[:, p, :], x1_ready)
                    dve.wait_ge(x1_ready, sum(diagonal(u) and STEPS[u][1] > 0 for u in range(s + 1)))
                v.bn_stats(stats2[:, p, :], x1).then_inc(stat2, 1)
                dve.wait_ge(stat2, n)
                v.bn_aggr(mean_var2[:, p, :], stats2[:, p, :]).then_inc(var2_ready, 1)

            def h_part(s):
                G, c, p = STEPS[s]
                dve.wait_ge(rstd2_ready, TG * G + p + 1)
                if G > 0 and p == 0:
                    dve.wait_ge(hT_ready, KC * G)
                v.tensor_scalar(h_row[:, p, :], x_in[:, G % NX, p, :], mean_var2[:, p, 0:1], rstd2[:, p:p + 1],
                                ALU.subtract, ALU.mult).then_inc(h_ready, 1)

            def mix_part(J, j):
                (G, t0, n), r = JOBS[J], span(J)
                h, om = j % KC, (OM_K, OM_R)[j // KC]
                dve.wait_ge(mu_done, KC * J + h + 1)
                if j == 0:
                    dve.wait_ge(prev_ready, G + 1)
                    if J == 0:
                        dve.wait_ge(om_ready, 1)
                v.scalar_tensor_tensor(mix[:, j, r], hT[:, h, r], cols[:, om, h:h + 1], mix[:, j, r],
                                       ALU.mult, ALU.add).then_inc(mixed, 1)
                if j == 2 * KC - 1 and G + 1 < NG:
                    dve.wait_ge(mixed, 2 * KC * (J + 1))
                    if (G + 1) % GB == 0:
                        v.memset(hT[:, :, 0:1], 0.0).then_inc(prev_ready, 1)
                    else:
                        v.tensor_copy(hT[:, :, 0:1], hT[:, :, GW:GW + 1]).then_inc(prev_ready, 1)

            def mix_low(J, j):
                r = span(J)
                dve.wait_ge(mix_high, 2 * KC * J + j + 1)
                low(mix_lo[:, j, r], mix[:, j, r], mix_hi[:, j, r], mix_split)

            def act_low(J, h):
                r = span(J)
                dve.wait_ge(act_high, KC * J + h + 1)
                low(act_lo[:, h, r], act[:, h, r], act_hi[:, h, r], act_split)

            def ff_part(J, i):
                n, t = pair(J, i) + 1, JOBS[J][1] + 2 * i
                dve.wait_ge(gate_ready, n)
                dve.wait_ge(ff_ready, n)
                rows = gate[:, t:t + 2, :].rearrange("p t c -> p (t c)")
                v.scalar_tensor_tensor(rows, rows, 1.0, bank_of("ff", J, i)[:], ALU.add, ALU.mult).then_inc(ff_used, 1)

            def last_ff_part():
                G, t0, n = JOBS[LAST]
                dve.wait_ge(gate_ready, 2 * NG)
                for i in range(n):
                    dve.wait_ge(last_ff_ready, i + 1)
                    v.scalar_tensor_tensor(gate[:, t0 + i, :], gate[:, t0 + i, :], 1.0,
                                           bank_s[i][:, 0:C], ALU.add, ALU.mult).then_inc(last_gated, 1)
                    dve.wait_ge(last_gated, i + 1)
                    v.tensor_tensor(gate[:, t0 + i, :], gate[:, t0 + i, :], x_in[:, G % NX, t0 + i, :], ALU.add)\
                        .then_inc(last_out_ready, 1)

            for s in SLOTS:
                if s + 2 < NS:
                    scores(s + 2)
                if diagonal(s - 2):
                    h_part(s - 2)
                if diagonal(s - 1):
                    x1_part(s - 1)
                if 0 <= s + 1 < NS:
                    pT_part(s + 1)
                for stage, n, i in STAGES[s]:
                    if stage == "stats":
                        ln1_stats(n, i)
                    elif stage == "xT":
                        xT_part(n, i)
                    elif stage == "kT":
                        kT_part(n, i)
                    elif stage == "v":
                        v_part(n, i)
                    elif stage == "apply":
                        ln1_apply(n, i)
                    elif stage == "dot":
                        e_dot(n, i)
                    elif stage == "mix":
                        mix_part(n, i)
                        if n == LAST and i > 0:
                            mix_low(n, i - 1)
                        if n == LAST and i == 2 * KC - 1:
                            mix_low(n, i)
                    elif stage == "kk" and n == LAST:
                        act_low(n, i)
                    elif stage == "ff" and n == LAST:
                        last_ff_part()
                    elif stage == "ff":
                        ff_part(n, i)
                if 0 <= s < NS:
                    o_part(s)

        @block.tensor
        def _(pe):
            mm = nc.tensor.matmul

            def product(dst, parts, then=None):
                last = None
                for n, (a_hi, a_lo, b_hi, b_lo) in enumerate(parts):
                    end = n == len(parts) - 1
                    mm(dst, a_hi, b_hi, start=n == 0, stop=False)
                    if then and n == 0:
                        mm(then[0], then[1], then[2], start=False, stop=False)
                    mm(dst, a_hi, b_lo, start=False, stop=False)
                    last = mm(dst, a_lo, b_hi, start=False, stop=end)
                return last

            def project(dst, w_hi, w_lo, cols_, x_hi, x_lo):
                return product(dst, [(w_hi[:, k, cols_], w_lo[:, k, cols_], x_hi[:, k, :], x_lo[:, k, :]) for k in range(KC)])

            def by_rows(dst, i, x_hi, x_lo, w_hi, w_lo):
                for t in range(2 * i, 2 * i + 2):
                    rows = slice(t * P, (t + 1) * P)
                    last = product(dst[:, (t % 2) * C:(t % 2 + 1) * C],
                                   [(x_hi[:, k, rows], x_lo[:, k, rows], w_hi[:, k, :], w_lo[:, k, :]) for k in range(KC)])
                return last

            def free(*use):
                n = USES.index(use)
                if n < 2:
                    return
                stage, g, i = USES[n - 2]
                if stage == "e":
                    pe.wait_ge(e_copied, g + 1)
                elif stage in ("rr", "ff"):
                    pe.wait_ge({"rr": gate_ready, "ff": ff_used}[stage], pair(g, i) + 1)
                else:
                    pe.wait_ge({"xT": xT_split, "kT": kT_split, "v": v_split, "hT": mu_done, "kk": k_relu}[stage], 2 * g + i + 1)

            def transposes(bank, src, h, tiles):
                for t in tiles:
                    last = nc.tensor.transpose(bank[:, t * P:(t + 1) * P], src[:, t, h * P:(h + 1) * P], ident[:])
                return last

            def xT(G, h):
                free("xT", G, h)
                pe.wait_ge(xhat_ready, TG * (G + 1))
                transposes(bank_of("xT", G, h), xhat, h, range(TG)).then_inc(xT_ready, 1)

            def kT(G, h):
                free("kT", G, h)
                pe.wait_ge(xT_split, KC * (G + 1))
                project(bank_of("kT", G, h)[:], wkq_hi, wkq_lo, slice(h * P, (h + 1) * P),
                        xT_hi[:, G % NT], xT_lo[:, G % NT]).then_inc(kT_ready, 1)

            def vv(G, i):
                free("v", G, i)
                by_rows(bank_of("v", G, i), i, xT_hi[:, G % NT], xT_lo[:, G % NT], wvo_hi, wvo_lo).then_inc(v_ready, 1)

            def e(G):
                free("e", G, 0)
                pe.wait_ge(dotted, TG * (G + 1))
                bank = bank_of("e", G, 0)
                for t in range(TG):
                    last = nc.tensor.transpose(bank[:, t * P:(t + 1) * P], e_col[:, t:t + 1].to_broadcast([P, P]), ident[:])
                last.then_inc(e_ready, 1)

            def hTr(J, h):
                G, t0, n = JOBS[J]
                free("hT", J, h)
                pe.wait_ge(h_ready, TG * G + t0 + n)
                transposes(bank_of("hT", J, h), h_row, h, range(t0, t0 + n)).then_inc(hT_ready, 1)

            def kk(J, h):
                r = span(J)
                free("kk", J, h)
                pe.wait_ge(mix_split, 2 * KC * J + KC)
                project(bank_of("kk", J, h)[:, r], ffn_hi[:, 0], ffn_lo[:, 0], slice(h * P, (h + 1) * P),
                        mix_hi[:, 0:KC, r], mix_lo[:, 0:KC, r]).then_inc(k_ready, 1)

            def rr(J, i):
                free("rr", J, i)
                pe.wait_ge(mix_split, 2 * KC * (J + 1))
                by_rows(bank_of("rr", J, i), JOBS[J][1] // 2 + i, mix_hi[:, KC:], mix_lo[:, KC:], ffn_hi[:, 1], ffn_lo[:, 1])\
                    .then_inc(r_ready, 1)

            def ff(J, i):
                free("ff", J, i)
                pe.wait_ge(act_split, KC * (J + 1))
                by_rows(bank_of("ff", J, i), JOBS[J][1] // 2 + i, act_hi, act_lo, ffn_hi[:, 2], ffn_lo[:, 2]).then_inc(ff_ready, 1)

            def last_ff():
                G, t0, n = JOBS[LAST]
                pe.wait_ge(act_split, KC * (LAST + 1))
                pe.wait_ge(s_used, NS)
                for i in range(n):
                    rows = slice((t0 + i) * P, (t0 + i + 1) * P)
                    product(bank_s[i][:, 0:C], [(act_hi[:, k, rows], act_lo[:, k, rows], ffn_hi[:, 2, k, :], ffn_lo[:, 2, k, :])
                                                for k in range(KC)]).then_inc(last_ff_ready, 1)

            def keep_warm(n):
                for _ in range(n):
                    mm(bank_p[0][:], ffn_hi[:, 0, 0, 0:P], kT_hi[:, 0, 0:GW], start=True, stop=True)

            def scores(s):
                G, c, p = STEPS[s]
                rows = slice(p * P, (p + 1) * P)
                keys = slice(c * GW, c * GW + max(width(s), 2 * P))
                if s >= 2:
                    pe.wait_ge(s_used, s - 1)
                if p == 0:
                    pe.wait_ge(xT_split, KC * (G + 1))
                bank, mask = bank_s[s % 2], None
                if diagonal(s):
                    if p == 0:
                        pe.wait_ge(kT_split, KC * (G + 1))
                    mask = (bank[:, rows], ident_b[:], mask_b[:])
                product(bank[:, 0:keys.stop - keys.start],
                        [(xT_hi[:, G % NT, k, rows], xT_lo[:, G % NT, k, rows], kT_hi[:, k, keys], kT_lo[:, k, keys])
                         for k in range(KC)], mask).then_inc(s_ready, 1)

            def pT(s):
                pe.wait_ge(exp_done, s + 1)
                for b in range(width(s) // P):
                    last = nc.tensor.transpose(bank_p[s % 2][:, b * P:(b + 1) * P], prob[:, s % 2, b * P:(b + 1) * P], ident[:])
                last.then_inc(pT_ready, 1)

            def pv(s):
                G, c, p = STEPS[s]
                pe.wait_ge(pT_split, s + 1)
                if s >= 2:
                    pe.wait_ge(o_added, s - 1)
                if diagonal(s) and p == 0:
                    pe.wait_ge(v_split, 2 * (G + 1))
                product(bank_o[s % 2][:, 0:C],
                        [(pT_hi[:, s % 2, b * P:(b + 1) * P], pT_lo[:, s % 2, b * P:(b + 1) * P],
                          v_hi[:, c * TG + b, :], v_lo[:, c * TG + b, :]) for b in range(width(s) // P)])\
                    .then_inc(o_ready, 1)

            pe.wait_ge(const_ready, 7)
            def transposed(raw, bank):
                for d in range(KC):
                    for k in range(KC):
                        last = nc.tensor.transpose(bank[:, d * C + k * P:d * C + (k + 1) * P], raw[:, k, d * P:(d + 1) * P], ident[:])
                last.then_inc(fold_ready, 1)

            def transposed_ffn(i):
                for k in range(KC):
                    for d in range(KC):
                        last = nc.tensor.transpose(ffn_bank[i][:, k * C + d * P:k * C + (d + 1) * P],
                                                   raw_ffn[:, i, d, k * P:(k + 1) * P], ident[:])
                last.then_inc(ffn_ready, 1)

            pe.wait_ge(wk_loaded, 16)
            transposed(raw_k, bank_p[0])
            pe.wait_ge(wq_loaded, 16)
            transposed(raw_q, bank_p[1])
            pe.wait_ge(fold_moved, 2)
            for h in range(KC):
                for d in range(KC):
                    last = mm(bank_s[1][:, h * C:(h + 1) * C], wkT[:, d, h * P:(h + 1) * P], wqT[:, d, :], start=d == 0, stop=d == KC - 1)
            last.then_inc(fold_ready, 1)
            pe.wait_ge(wv_loaded, 16)
            transposed(raw_v, bank_s[0])
            for h in range(KC):
                xT(0, h)
            pe.wait_ge(fold_moved, 4)
            pe.wait_ge(wo_loaded, 16)
            for h in range(KC):
                for d in range(KC):
                    last = mm(bank_o[h][:, 0:C], wvT[:, d, h * P:(h + 1) * P], raw_o[:, d, :], start=d == 0, stop=d == KC - 1)
            last.then_inc(fold_ready, 1)
            pe.wait_ge(ffn_loaded, 48)
            pe.wait_ge(fold_split, 1)
            transposed_ffn(0)
            transposed_ffn(1)
            pe.wait_ge(col_loaded, 80)
            for h in range(KC):
                for d in range(KC):
                    last = mm(bank_p[0][:, h:h + 1], wqT[:, d, h * P:(h + 1) * P], cols[:, BK, d:d + 1],
                              start=d == 0, stop=d == KC - 1)
            for d in range(KC):
                last = mm(bank_p[0][:, KC:KC + 1], cols[:, BK, d:d + 1].to_broadcast([P, P]), cols[:, BQ, d:d + 1],
                          start=d == 0, stop=d == KC - 1)
            for d in range(KC):
                last = mm(bank_p[0][:, C:2 * C], cols[:, BQ, d:d + 1].to_broadcast([P, P]), wkT[:, d, :],
                          start=d == 0, stop=d == KC - 1)
            last.then_inc(fold_ready, 1)
            for d in range(KC):
                last = mm(bank_p[1][:, 0:C], cols[:, BV, d:d + 1].to_broadcast([P, P]), raw_o[:, d, :], start=d == 0, stop=d == KC - 1)
            last.then_inc(fold_ready, 1)
            pe.wait_ge(fold_split, 3)
            for h in range(KC):
                kT(0, h)
            for i in range(2):
                vv(0, i)
            transposed_ffn(2)
            e(0)

            for s in SLOTS:
                if s in (-2, 0):
                    pe.wait_ge(ffn_split, 2 if s == -2 else 3)
                if s + 2 < NS:
                    scores(s + 2)
                if s == -1:
                    pe.wait_ge(bias_ready, 1)
                if 0 <= s + 1 < NS:
                    pT(s + 1)
                if s == HT_AT[LAST][0]:
                    pe.wait_ge(pT_split, NS)
                    keep_warm(4)
                if s == KK_AT[LAST][0]:
                    pe.wait_ge(mu_done, KC * LAST + 2)
                    keep_warm(3)
                for stage, n, i in STAGES[s]:
                    if stage == "xT":
                        xT(n, i)
                    elif stage == "kT":
                        kT(n, i)
                    elif stage == "v":
                        vv(n, i)
                    elif stage == "e":
                        e(n)
                    elif stage == "hT":
                        hTr(n, i)
                    elif stage == "kk":
                        kk(n, i)
                    elif stage == "rr":
                        rr(n, i)
                    elif stage == "ff" and n == LAST:
                        last_ff()
                    elif stage == "ff":
                        ff(n, i)
                if 0 <= s < NS:
                    pv(s)


_INS = ["L0_attn_y_all", "L0_attn_Wq", "L0_attn_bq", "L0_attn_Wk", "L0_attn_bk", "L0_attn_Wv", "L0_attn_bv", "L0_attn_Wo",
        "L0_attn_bo", "L0_ffn_W_r", "L0_ffn_W_k", "L0_ffn_W_v", "L0_ffn_mu_r", "L0_ffn_mu_k"]


def kernel(**inputs):
    import numpy as _np
    import concourse.bacc as _bacc
    from concourse import mybir as _mybir
    from concourse.bass_utils import run_bass_kernel_spmd as _run

    nc = _bacc.Bacc("TRN2", target_bir_lowering=False, num_devices=1)
    arrays, args = {}, []
    for name in _INS:
        a = _np.ascontiguousarray(inputs[name])
        arrays[f"in_{name}_dram"] = a
        args.append(nc.dram_tensor(f"in_{name}_dram", a.shape, _mybir.dt.from_np(a.dtype), kind="ExternalInput").ap())
    shape = arrays["in_L0_attn_y_all_dram"].shape
    args.append(nc.dram_tensor("out_0_dram", shape, _mybir.dt.float32, kind="ExternalOutput").ap())
    attention_channel_mix_block(nc, *args)
    r = _run(nc, [arrays], core_ids=[0])
    return r.results[0]["out_0_dram"]
```
